# Optimizing a Trainium2 kernel written in Bass

```python
import numpy as np
import jax
import jax.numpy as jnp

def _softmax(x, axis=-1):
    return jax.nn.softmax(x, axis=axis)

def _gelu(x):
    return jax.nn.gelu(x, approximate=True)

def _silu(x):
    return jax.nn.silu(x)

def _sigmoid(x):
    return jax.nn.sigmoid(x)

def _layernorm(x, axis=-1, eps=1e-05):
    m = jnp.mean(x, axis=axis, keepdims=True)
    v = jnp.var(x, axis=axis, keepdims=True)
    return (x - m) / jnp.sqrt(v + eps)

def _scatter_add(tgt, idx, src, axis=0):
    return tgt.at[idx].add(src)

def _segment_sum(src, seg, n):
    return jax.ops.segment_sum(src, seg, n)
kernel_name = 'mk_adj_resnorm_d2_adj_r2_fd17ea'

def setup_inputs(seed: int=0):
    np.random.seed(seed)
    _w = jnp.asarray

    def _rec_inputs():
        import jax
        import jax.numpy as jnp
        _gk = jax.random.key(seed)
        x = -0.000125 + 0.9999 * jax.random.normal(jax.random.fold_in(_gk, 1), (8, 1024, 256), jnp.float32)
        _a = jax.random.bernoulli(jax.random.fold_in(_gk, 2), 0.00390625, (1024, 1024))
        _af = _a.astype(jnp.float32)
        adj = _af
        return (x, adj)
    x, adj = _rec_inputs()

    def _L0_gnn_setup():
        import jax, jax.numpy as jnp
        import numpy as np
        ALPHA = 0.2
        key = jax.random.key(seed)
        k0, k1, k2, k3 = jax.random.split(key, 4)
        B, N, C, F = (64, 512, 256, 256)
        x = jax.random.normal(k0, (B, N, C), dtype=jnp.float32)
        W = jax.random.normal(k1, (C, F), dtype=jnp.float32) * (1.414 / np.sqrt(C + F))
        a = jax.random.normal(k2, (2 * F, 1), dtype=jnp.float32) * (1.414 / np.sqrt(2 * F + 1))
        beta = jnp.ones((1,), dtype=jnp.float32)
        mask = (jax.random.uniform(k3, (N, N)) < 0.3).astype(jnp.float32)
        return {'x': x, 'W': W, 'a': a, 'beta': beta, 'mask': mask}
    _L0_gnn_all = _L0_gnn_setup()
    _L0_gnn_in = {k: v for k, v in _L0_gnn_all.items() if k in ('W', 'a', 'beta')}
    del _L0_gnn_all

    def _L1_gnn_setup():
        import jax, jax.numpy as jnp
        import numpy as np
        B, N, F_IN, F_OUT = (16, 1024, 256, 256)
        key = jax.random.key(seed)
        k1, k2, k3 = jax.random.split(key, 3)
        x = jax.random.normal(k1, (B, N, F_IN), dtype=jnp.float32)
        adj = jax.random.uniform(k2, (N, N), dtype=jnp.float32)
        bound = np.sqrt(6.0 / F_OUT)
        weight = jax.random.uniform(k3, (F_IN, F_OUT), dtype=jnp.float32, minval=-bound, maxval=bound)
        bias = jnp.zeros((F_OUT,), dtype=jnp.float32)
        return {'x': x, 'adj': adj, 'weight': weight, 'bias': bias}
    _L1_gnn_all = _L1_gnn_setup()
    _L1_gnn_in = {k: v for k, v in _L1_gnn_all.items() if k in ('weight', 'bias')}
    del _L1_gnn_all
    return {'x': x, 'adj': adj, 'L0_gnn_W': _L0_gnn_in['W'], 'L0_gnn_a': _L0_gnn_in['a'], 'L0_gnn_beta': _L0_gnn_in['beta'], 'L1_gnn_weight': _L1_gnn_in['weight'], 'L1_gnn_bias': _L1_gnn_in['bias']}

def reference(x, adj, L0_gnn_W, L0_gnn_a, L0_gnn_beta, L1_gnn_weight, L1_gnn_bias):
    import jax
    import jax.numpy as jnp

    def _L0_gnn_ref(x, W, a, beta, mask):
        import jax, jax.numpy as jnp
        import numpy as np
        ALPHA = 0.2
        F_ = W.shape[1]
        h = jnp.einsum('bnc,cf->bnf', x, W)
        a1, a2 = (a[:F_, 0], a[F_:, 0])
        s1 = jnp.einsum('bnf,f->bn', h, a1)
        s2 = jnp.einsum('bnf,f->bn', h, a2)
        e = jax.nn.leaky_relu(s1[:, :, None] + s2[:, None, :], negative_slope=ALPHA)
        e = e * mask[None, :, :]
        att = jax.nn.softmax(e, axis=2)
        h_prime = jnp.einsum('bij,bjf->bif', att, h)
        return jax.nn.elu(h_prime + beta * h)

    def _L1_gnn_ref(x, adj, weight, bias):
        import jax, jax.numpy as jnp
        import numpy as np
        B, N, F_IN, F_OUT = (16, 1024, 256, 256)
        deg = adj.sum(axis=1)
        deg_inv_sqrt = jnp.where(deg > 0, jax.lax.rsqrt(deg), 0.0)
        norm_adj = adj * deg_inv_sqrt[:, None] * deg_inv_sqrt[None, :]
        support = jnp.einsum('bni,io->bno', x, weight)
        output = jnp.einsum('nm,bmo->bno', norm_adj, support)
        return output + bias
    x = _layernorm(x + _L0_gnn_ref(x, L0_gnn_W, L0_gnn_a, L0_gnn_beta, adj), axis=-1)
    x = _layernorm(x + _L1_gnn_ref(x, adj, L1_gnn_weight, L1_gnn_bias), axis=-1)
    return x

_drawn_inputs = setup_inputs


def setup_inputs(seed=0):
    import zlib

    import numpy as np

    out = dict(_drawn_inputs(seed))
    spreads = {'L1_gnn_bias': (0.0, 0.1)}
    factors = {'L0_gnn_a': 6.23}
    for name, (base, spread) in spreads.items():
        noise = np.random.default_rng([zlib.crc32(name.encode()), seed]).standard_normal(out[name].shape)
        drawn = base * np.exp(spread * noise) if base else spread * noise
        out[name] = jnp.asarray(drawn.astype(out[name].dtype))
    for name, factor in factors.items():
        out[name] = (out[name] * factor).astype(out[name].dtype)
    return out
```

```python
from contextlib import ExitStack

import concourse.bass as bass
import concourse.mybir as mybir

F32 = mybir.dt.float32
F32R = mybir.dt.float32r
ALU = mybir.AluOpType
ACT = mybir.ActivationFunctionType
AXX = mybir.AxisListType.X

P = 128
B, N, D = 8, 1024, 256
T = N // P
C = D // P
NT = B * T
HC = D + 2
HP = D + 4
PAIRS = T // 2
HALF = T // 2 * P
SLOPE = 0.2
EPS = 1e-5
TINY = 1.2e-38
ZR = 4
SR = 4
XS = 2 * T


def build(nc, x, xT, adj, adjT, W0, a, beta, W1, bias, out):
    with ExitStack() as ctx:
        def sb(name, shape, dt=F32):
            return ctx.enter_context(nc.sbuf_tensor(name, shape, dt))

        def pb(name):
            return ctx.enter_context(nc.psum_tensor(name, [P, 512], F32))

        def sem(name):
            return ctx.enter_context(nc.semaphore(name))

        adj_sb = sb("adj_sb", [P, T, N])
        adjT_hi = sb("adjT_hi", [P, T, N], F32R)
        adjT_lo = sb("adjT_lo", [P, T, N], F32R)
        w0_hi = sb("w0_hi", [P, C, HC], F32R)
        w0_lo = sb("w0_lo", [P, C, HC], F32R)
        w1_hi = sb("w1_hi", [P, C, D], F32R)
        w1_lo = sb("w1_lo", [P, C, D], F32R)
        ident = sb("ident", [P, P])
        beta_ident = sb("beta_ident", [P, P])
        bias_bc = sb("bias_bc", [P, D])
        beta_bc = sb("beta_bc", [P, 1])
        deg = sb("deg", [P, T])
        deg_pos = sb("deg_pos", [P, T])
        dis = sb("dis", [P, T])
        neg_half = sb("neg_half", [P, T])
        xT_sb = sb("xT_sb", [P, 2, C, 2 * P])
        xs_hi = sb("xs_hi", [P, 2, C, 2 * P], F32R)
        xs_lo = sb("xs_lo", [P, 2, C, 2 * P], F32R)
        h_hi = sb("h_hi", [P, 2, T, HP], F32R)
        h_lo = sb("h_lo", [P, 2, T, HP], F32R)
        s12 = sb("s12", [P, 2, T, 2])
        s2b = sb("s2b", [P, N])
        score = sb("score", [P, ZR, N])
        row_max = sb("row_max", [P, SR])
        neg_max = sb("neg_max", [P, SR])
        row_sum = sb("row_sum", [P, SR])
        inv_sum = sb("inv_sum", [P, SR])
        pt_hi = sb("pt_hi", [P, T, P], F32R)
        pt_lo = sb("pt_lo", [P, T, P], F32R)
        elu = sb("elu", [P, 2, D])
        stats = sb("stats", [P, SR, 6])
        mv = sb("mv", [P, SR, 2])
        var_eps = sb("var_eps", [P, SR])
        rstd = sb("rstd", [P, SR])
        x1 = sb("x1", [P, XS, D])
        x1t_hi = sb("x1t_hi", [P, C * P], F32R)
        x1t_lo = sb("x1t_lo", [P, C * P], F32R)
        sup_hi = sb("sup_hi", [P, 2, D], F32R)
        sup_lo = sb("sup_lo", [P, 2, D], F32R)
        o_stats = sb("o_stats", [P, 2, 6])
        o_mv = sb("o_mv", [P, 2, 2])
        o_var_eps = sb("o_var_eps", [P, 2])
        o_rstd = sb("o_rstd", [P, 2])
        v12 = sb("v12", [P, C, 2])
        w0_raw = score[:, 3, 0:C * D].rearrange("p (c d) -> p c d", c=C)
        a_bc = score[:, 3, C * D:C * D + 2 * D]
        w1_raw = score[:, 2, 0:C * D].rearrange("p (c d) -> p c d", c=C)
        products = score[:, 1, :].rearrange("p (v d) -> p v d", v=2 * C)
        adjT_raw = [x1[:, T + 4 * k:T + 4 * k + 4, :].rearrange("p s d -> p (s d)") for k in range(2)]

        bank_pt = [pb("bank_pt0"), pb("bank_pt1")]
        bank_att = pb("bank_att")
        bank_mix = pb("bank_mix")
        bank_acc = [pb(f"bank_acc{i}") for i in range(4)]

        x_in = [sem(f"x_in{s}") for s in range(XS // 2)]
        out_done = [sem(f"out_done{s}") for s in range(XS // 2)]
        xT_in = [sem(f"xT_in{q}") for q in range(2)]
        adj_in = [sem(f"adj_in{t}") for t in range(T)]
        adjT_in = [sem(f"adjT_in{k}") for k in range(2)]
        w0_in, w1_in, bias_in, beta_in, a_in = (
            sem("w0_in"), sem("w1_in"), sem("bias_in"), sem("beta_in"), sem("a_in"))
        const_done = sem("const_done")
        v_done, w0_rounded, w1_rounded, w_split = sem("v_done"), sem("w0_rounded"), sem("w1_rounded"), sem("w_split")
        beta_done = sem("beta_done")
        adjT_rounded, adjT_split = sem("adjT_rounded"), sem("adjT_split")
        deg_done, deg_clamped, deg_rooted, dis_ready = (
            sem("deg_done"), sem("deg_clamped"), sem("deg_rooted"), sem("dis_ready"))
        x_rounded, x_split = sem("x_rounded"), sem("x_split")
        h_done, h_rounded, h_split = sem("h_done"), sem("h_rounded"), sem("h_split")
        s_ready, s2row_done, s2b_ready = sem("s_ready"), sem("s2row_done"), sem("s2b_ready")
        z_ready, leaky_done, max_done, negmax_done = (
            sem("z_ready"), sem("leaky_done"), sem("max_done"), sem("negmax_done"))
        exp_done, prob_ready = sem("exp_done"), sem("prob_ready")
        pt_done, pt_rounded, pt_split = sem("pt_done"), sem("pt_rounded"), sem("pt_split")
        att_done, eu_done, em_done, elu_done = sem("att_done"), sem("eu_done"), sem("em_done"), sem("elu_done")
        r_done, stats_done, mv_done, ve_done = sem("r_done"), sem("stats_done"), sem("mv_done"), sem("ve_done")
        rstd_done, x1_ready, x1b_done = sem("rstd_done"), sem("x1_ready"), sem("x1b_done")
        x1t_done, x1t_rounded, x1t_split = sem("x1t_done"), sem("x1t_rounded"), sem("x1t_split")
        sup_done, sup_rounded, sup_split = sem("sup_done"), sem("sup_rounded"), sem("sup_split")
        acc_done, r2_done, ostats_done, omv_done, ove_done, orstd_done, result_ready = (
            sem("acc_done"), sem("r2_done"), sem("ostats_done"), sem("omv_done"), sem("ove_done"),
            sem("orstd_done"), sem("result_ready"))

        def wait(eng, signal, count):
            if not isinstance(count, int) or count > 0:
                eng.wait_ge(signal, count)

        def live(b, t, shift=0):
            return not isinstance(b, int) or 0 <= T * b + t + shift < NT

        def batch_live(b):
            return not isinstance(b, int) or 0 <= b < B

        def steps(eng, step):
            for b in (-1, 0):
                for t in range(T):
                    step(b, b // 2, b % 2, t)
            with eng.Fori(0, (B - 2) // 2) as i:
                for b, half, u in ((i * 2 + 1, i, 1), (i * 2 + 2, i + 1, 0)):
                    for t in range(T):
                        step(b, half, u, t)
            for b in (B - 1, B):
                for t in range(T):
                    step(b, b // 2, b % 2, t)

        def slot(u, t, shift=0):
            return (T * u + t + shift) % XS

        def adjT_step(b, t):
            g = T * b + t + T // 2 if isinstance(b, int) else -1
            return g if 0 <= g < T else None

        block = ctx.enter_context(nc.Block())

        @block.sync
        def _(sp):
            def load_xT(b, q):
                m = b * PAIRS + q
                wait(sp, x_split, m - 1)
                sp.dma_start(xT_sb[:, q % 2, :, :], xT[m]).then_inc(xT_in[q % 2], 16)

            def load_x(b, u, q):
                s = slot(u, 2 * q)
                sp.dma_start(x1[:, s:s + 2, :], x[b * PAIRS + q]).then_inc(x_in[s // 2], 16)

            def round_(b, half_before, u):
                for c, q in ((b + 1, 2), (b + 1, 3), (b + 2, 0), (b + 2, 1)):
                    if batch_live(c):
                        load_xT(c, q)
                for q in range(PAIRS):
                    s = slot(1 - u, 2 * q)
                    if batch_live(b - 1):
                        sp.wait_ge(result_ready, (b - 1) * PAIRS + q + 1)
                        sp.dma_start(out[(b - 1) * PAIRS + q], x1[:, s:s + 2, :]).then_inc(out_done[s // 2], 16)
                for q in range(PAIRS):
                    s = slot(1 - u, 2 * q)
                    if batch_live(b - 1) and batch_live(b + 1):
                        sp.wait_ge(out_done[s // 2], (half_before + 1) * 16)
                        load_x(b + 1, 1 - u, q)

            load_xT(0, 0)
            sp.dma_start(w0_raw, W0).then_inc(w0_in, 16)
            sp.dma_start(a_bc, a.to_broadcast([P, 2 * D])).then_inc(a_in, 16)
            load_xT(0, 1)
            sp.dma_start(beta_bc[:, :], beta.to_broadcast([P, 1])).then_inc(beta_in, 16)
            sp.dma_start(w1_raw, W1).then_inc(w1_in, 16)
            sp.dma_start(bias_bc[:, :], bias.to_broadcast([P, D])).then_inc(bias_in, 16)
            for t in range(3):
                sp.dma_start(adj_sb[:, t, :], adj[t]).then_inc(adj_in[t], 16)
            load_xT(0, 2)
            load_xT(0, 3)
            for t in range(3, T):
                sp.dma_start(adj_sb[:, t, :], adj[t]).then_inc(adj_in[t], 16)
            for k in range(2):
                sp.dma_start(adjT_raw[k], adjT[k]).then_inc(adjT_in[k], 16)
            load_x(0, 0, 0)
            load_xT(1, 0)
            load_xT(1, 1)
            for k in range(2, T):
                sp.wait_ge(adjT_split, k - 1)
                sp.dma_start(adjT_raw[k % 2], adjT[k]).then_inc(adjT_in[k % 2], 16)
                if k < PAIRS + 1:
                    load_x(0, 0, k - 1)
                if k in (T - 3, T - 2):
                    load_xT(1, k - T + 5)
            sp.wait_ge(adjT_split, T)
            for q in range(PAIRS):
                load_x(1, 1, q)
            load_xT(2, 0)
            load_xT(2, 1)
            with sp.Fori(0, (B - 4) // 2) as i:
                round_(i * 2 + 1, i, 1)
                round_(i * 2 + 2, i, 0)
            for b in range(B - 3, B + 1):
                round_(b, (b - 1) // 2, b % 2)
            for s in range(XS // 2):
                sp.wait_ge(out_done[s], 16 * (B // 2))

        @block.gpsimd
        def _(pool):
            pool.memset(neg_half[:, :], -0.5)
            pool.memset(ident[:, :], 0.0).then_inc(const_done, 1)
            pool.wait_ge(const_done, 1)
            pool.affine_select(out=ident[:, :], in_=ident[:, :], compare_op=ALU.not_equal, fill=1.0, base=0,
                               pattern=[[-1, P]], channel_multiplier=1).then_inc(const_done, 1)
            pool.wait_ge(const_done, 2)

            def split_x(b, q):
                m = b * PAIRS + q
                pool.wait_ge(x_rounded, m + 1)
                pool.tensor_tensor(xs_lo[:, q % 2, :, :], xT_sb[:, q % 2, :, :],
                                   xs_hi[:, q % 2, :, :].bitcast(F32), ALU.subtract).then_inc(x_split, 1)

            def step(b, half, u, t):
                n = b * T + t
                if batch_live(b + 1) and t < 3:
                    for q in ((0, 1) if t == 0 else (t + 1,)):
                        split_x(b + 1, q)
                if live(b, t, -1):
                    k = (t - 1) % SR
                    pool.wait_ge(ve_done, n)
                    pool.tensor_tensor(rstd[:, k:k + 1], var_eps[:, k:k + 1], neg_half[:, 0:1],
                                       ALU.pow).then_inc(rstd_done, 1)
                if live(b, t, -2):
                    s = slot(u, t, -2)
                    pool.wait_ge(x1t_done, n - 1)
                    if isinstance(b, int) and n == 2:
                        pool.wait_ge(bias_in, 16)
                    pool.tensor_tensor(x1[:, s, :], x1[:, s, :], bias_bc[:, :], ALU.add).then_inc(x1b_done, 1)
                if live(b, t):
                    s = slot(u, t)
                    pool.wait_ge(x_in[s // 2], (half + 1) * 16)
                    pool.wait_ge(elu_done, n + 1)
                    pool.tensor_tensor(x1[:, s, :], x1[:, s, :], elu[:, t % 2, :], ALU.add).then_inc(r_done, 1)
                if batch_live(b - 1) and t >= 4:
                    pool.wait_ge(ove_done, (b - 1) * PAIRS + t - 3)
                    pool.tensor_tensor(o_rstd[:, :], o_var_eps[:, :], neg_half[:, 0:2],
                                       ALU.pow).then_inc(orstd_done, 1)
                if isinstance(b, int) and b == -1 and t == T - 1:
                    pool.wait_ge(deg_clamped, 1)
                    pool.tensor_tensor(dis[:, :], deg[:, :], neg_half[:, :], ALU.pow).then_inc(deg_rooted, 1)

            steps(pool, step)

        @block.scalar
        def _(act):
            act.wait_ge(w0_in, 16)
            nc.scalar.activation(w0_hi[:, :, 0:D], w0_raw, ACT.Copy).then_inc(w0_rounded, 1)
            act.wait_ge(v_done, 1)
            nc.scalar.activation(w0_hi[:, :, D:HC], v12[:, :, :], ACT.Copy).then_inc(w0_rounded, 1)
            act.wait_ge(w1_in, 16)
            nc.scalar.activation(w1_hi[:, :, :], w1_raw, ACT.Copy).then_inc(w1_rounded, 1)

            def round_h(b, par, j):
                act.wait_ge(h_done, b * T + j + 1)
                nc.scalar.activation(h_hi[:, par, j, 0:HC], bank_mix[:, 0:HC], ACT.Copy).then_inc(h_rounded, 1)

            def copy_s2(b, i):
                if i == 0:
                    wait(act, z_ready, b * T)
                act.wait_ge(s2row_done, b * 2 + i + 1)
                nc.scalar.activation(s2b[:, i * HALF:(i + 1) * HALF], bank_mix[:, :], ACT.Copy).then_inc(s2b_ready, 1)

            def step(b, half, u, t):
                n = b * T + t
                if live(b, t, -2):
                    act.wait_ge(x1t_done, n - 1)
                    nc.scalar.activation(x1t_hi[:, :], bank_mix[:, 0:D], ACT.Copy).then_inc(x1t_rounded, 1)
                if live(b, t, 3):
                    tz = (t + 3) % T
                    par = u if t + 3 < T else 1 - u
                    if tz == 0:
                        act.wait_ge(s2b_ready, b * 2 + 4)
                    if isinstance(b, int) and n in (-1, 0):
                        act.wait_ge(w_split, 3)
                    wait(act, pt_done, n * 2)
                    nc.scalar.activation(score[:, (t + 3) % ZR, :], s2b[:, :], ACT.Identity,
                                         bias=s12[:, par, tz, 0:1]).then_inc(z_ready, 1)
                if batch_live(b + 1) and t < 4:
                    round_h(b + 1, 1 - u, 2 * t)
                if batch_live(b + 1) and t == 4:
                    copy_s2(b + 1, 0)
                if live(b, t):
                    act.wait_ge(att_done, n + 1)
                    wait(act, r_done, n - 1)
                    nc.scalar.activation(elu[:, t % 2, :], bank_att[:, 0:D], ACT.Exp,
                                         scale=inv_sum[:, t % SR:t % SR + 1]).then_inc(eu_done, 1)
                if live(b, t, -2):
                    k = (t - 2) % T
                    act.wait_ge(sup_done, n - 1)
                    if isinstance(b, int) and n == 2:
                        act.wait_ge(dis_ready, 1)
                    nc.scalar.activation(sup_hi[:, t % 2, :], bank_mix[:, 0:D], ACT.Copy,
                                         scale=dis[:, k:k + 1]).then_inc(sup_rounded, 1)
                if live(b, t, 1):
                    for i in range(2):
                        act.wait_ge(pt_done, n * 2 + 3 + i)
                        nc.scalar.activation(pt_hi[:, 4 * i:4 * i + 4, :], bank_pt[i][:, :].rearrange(
                            "p (k q) -> p k q", k=4), ACT.Copy).then_inc(pt_rounded, 1)
                if batch_live(b + 1) and t < 4:
                    round_h(b + 1, 1 - u, 2 * t + 1)
                if batch_live(b + 1) and t == 4:
                    copy_s2(b + 1, 1)
                if live(b, t, 2):
                    k = (t + 2) % SR
                    act.wait_ge(negmax_done, n + 3)
                    nc.scalar.activation(score[:, k % ZR, :], score[:, k % ZR, :], ACT.Exp,
                                         bias=neg_max[:, k:k + 1],
                                         accum_out=row_sum[:, k:k + 1]).then_inc(exp_done, 1)
                k = adjT_step(b, t)
                if k is not None:
                    act.wait_ge(adjT_in[k % 2], 16 * (k // 2 + 1))
                    nc.scalar.activation(adjT_hi[:, k, :], adjT_raw[k % 2], ACT.Copy).then_inc(adjT_rounded, 1)

            steps(act, step)

        @block.vector
        def _(dve):
            dve.memset(row_max[:, :], 0.0)
            dve.wait_ge(const_done, 2)
            dve.wait_ge(beta_in, 16)
            dve.tensor_scalar(beta_ident[:, :], ident[:, :], beta_bc[:, :], None, ALU.mult).then_inc(beta_done, 1)
            dve.wait_ge(w0_in, 16)
            dve.wait_ge(a_in, 16)
            for c in range(C):
                for j in range(2):
                    last = dve.tensor_tensor_reduce(out=products[:, 2 * c + j, :], in0=w0_raw[:, c, :], in1=a_bc[:, j * D:(j + 1) * D],
                                                    scale=1.0, scalar=0.0, op0=ALU.mult, op1=ALU.add,
                                                    accum_out=v12[:, c, j:j + 1])
            last.then_inc(v_done, 1)
            dve.wait_ge(w0_rounded, 1)
            dve.tensor_tensor(w0_lo[:, :, 0:D], w0_raw, w0_hi[:, :, 0:D].bitcast(F32), ALU.subtract).then_inc(w_split, 1)
            dve.wait_ge(w0_rounded, 2)
            dve.tensor_tensor(w0_lo[:, :, D:HC], v12[:, :, :], w0_hi[:, :, D:HC].bitcast(F32),
                              ALU.subtract).then_inc(w_split, 1)
            dve.wait_ge(w1_rounded, 1)
            dve.tensor_tensor(w1_lo[:, :, :], w1_raw, w1_hi[:, :, :].bitcast(F32), ALU.subtract).then_inc(w_split, 1)

            def round_x(b, q):
                m = b * PAIRS + q
                dve.wait_ge(xT_in[q % 2], (b * 2 + q // 2 + 1) * 16)
                wait(dve, h_done, (m - 1) * 2)
                dve.tensor_copy(xs_hi[:, q % 2, :, :], xT_sb[:, q % 2, :, :]).then_inc(x_rounded, 1)

            def split_h(b, par, j):
                dve.wait_ge(h_rounded, b * T + j + 1)
                dve.tensor_tensor(h_lo[:, par, j, 0:HC], bank_mix[:, 0:HC], h_hi[:, par, j, 0:HC].bitcast(F32),
                                  ALU.subtract).then_inc(h_split, 1)

            def residual(b, u, i):
                dve.wait_ge(x1b_done, b * T + T)
                dve.wait_ge(acc_done, b * 2 + i + 1)
                for j in range(4 * i, 4 * i + 4):
                    s = slot(u, j)
                    dve.scalar_tensor_tensor(out=x1[:, s, :], in0=bank_acc[j // 2][:, (j % 2) * D:(j % 2 + 1) * D],
                                             scalar=dis[:, j:j + 1], in1=x1[:, s, :], op0=ALU.mult,
                                             op1=ALU.add).then_inc(r2_done, 1)

            def step(b, half, u, t):
                n = b * T + t
                out_pair = batch_live(b - 1) and t >= 4
                if batch_live(b + 1) and t < 3:
                    for q in ((0, 1) if t == 0 else (t + 1,)):
                        round_x(b + 1, q)
                if out_pair:
                    for i in range(2):
                        s = slot(1 - u, 2 * (t - 4) + i)
                        dve.wait_ge(r2_done, b * T - T + 2 * (t - 4) + i + 1)
                        dve.bn_stats(o_stats[:, i, :], x1[:, s, :]).then_inc(ostats_done, 1)
                if live(b, t, -1):
                    dve.wait_ge(stats_done, n)
                if live(b, t, -2):
                    dve.wait_ge(x1t_rounded, n - 1)
                    dve.tensor_tensor(x1t_lo[:, :], bank_mix[:, 0:D], x1t_hi[:, :].bitcast(F32),
                                      ALU.subtract).then_inc(x1t_split, 1)
                if live(b, t, -1):
                    k = (t - 1) % SR
                    dve.bn_aggr(mv[:, k, :], stats[:, k, :]).then_inc(mv_done, 1)
                    dve.wait_ge(mv_done, n)
                    dve.tensor_scalar(var_eps[:, k:k + 1], mv[:, k, 1:2], EPS, None, ALU.add).then_inc(ve_done, 1)
                if live(b, t, 2):
                    k = (t + 2) % ZR
                    dve.wait_ge(z_ready, n + 3)
                    dve.scalar_tensor_tensor(out=score[:, k, :], in0=score[:, k, :], scalar=SLOPE,
                                             in1=score[:, k, :], op0=ALU.mult, op1=ALU.max).then_inc(leaky_done, 1)
                if batch_live(b + 1) and t < 4:
                    split_h(b + 1, 1 - u, 2 * t)
                if live(b, t, 2):
                    dve.wait_ge(leaky_done, n + 3)
                if live(b, t, -1):
                    k, s = (t - 1) % SR, slot(u, t, -1)
                    dve.wait_ge(rstd_done, n)
                    dve.tensor_scalar(x1[:, s, :], x1[:, s, :], mv[:, k, 0:1], rstd[:, k:k + 1],
                                      ALU.subtract, ALU.mult).then_inc(x1_ready, 1)
                if live(b, t, 2):
                    k = (t + 2) % SR
                    m = (t + 2) % T
                    if isinstance(b, int) and n + 2 < T:
                        dve.wait_ge(adj_in[m], 16)
                    dve.tensor_tensor_reduce(out=score[:, k % ZR, :], in0=score[:, k % ZR, :], in1=adj_sb[:, m, :],
                                             scale=1.0, scalar=-3.4e38, op0=ALU.mult, op1=ALU.max,
                                             accum_out=row_max[:, k:k + 1]).then_inc(max_done, 1)
                    dve.wait_ge(max_done, n + 3)
                    dve.tensor_scalar(neg_max[:, k:k + 1], row_max[:, k:k + 1], -1.0, None,
                                      ALU.mult).then_inc(negmax_done, 1)
                if live(b, t):
                    e = elu[:, t % 2, :]
                    dve.wait_ge(eu_done, n + 1)
                    dve.tensor_scalar(e, e, 1.0, -1.0, ALU.min, ALU.add).then_inc(em_done, 1)
                    dve.wait_ge(em_done, n + 1)
                    dve.scalar_tensor_tensor(out=e, in0=bank_att[:, 0:D], scalar=inv_sum[:, t % SR:t % SR + 1],
                                             in1=e, op0=ALU.mult, op1=ALU.max).then_inc(elu_done, 1)
                if live(b, t, -2):
                    k = (t - 2) % T
                    dve.wait_ge(sup_rounded, n - 1)
                    dve.scalar_tensor_tensor(out=sup_lo[:, t % 2, :], in0=bank_mix[:, 0:D], scalar=dis[:, k:k + 1],
                                             in1=sup_hi[:, t % 2, :].bitcast(F32), op0=ALU.mult,
                                             op1=ALU.subtract).then_inc(sup_split, 1)
                if batch_live(b - 1) and t == 3:
                    residual(b - 1, 1 - u, 1)
                if live(b, t, 1):
                    for i in range(2):
                        dve.wait_ge(pt_rounded, n * 2 + 3 + i)
                        dve.tensor_tensor(pt_lo[:, 4 * i:4 * i + 4, :], bank_pt[i][:, :].rearrange(
                            "p (k q) -> p k q", k=4), pt_hi[:, 4 * i:4 * i + 4, :].bitcast(F32),
                            ALU.subtract).then_inc(pt_split, 1)
                if batch_live(b + 1) and t < 4:
                    split_h(b + 1, 1 - u, 2 * t + 1)
                if batch_live(b + 1) and t == 3:
                    dve.wait_ge(h_split, b * T + 2 * T)
                    dve.tensor_tensor(s12[:, 1 - u, :, :], h_hi[:, 1 - u, :, D:HC].bitcast(F32),
                                      h_lo[:, 1 - u, :, D:HC].bitcast(F32), ALU.add).then_inc(s_ready, 1)
                if out_pair:
                    dve.wait_ge(ostats_done, b * T - T + 2 * (t - 4) + 2)
                if live(b, t, 2):
                    k, m = (t + 2) % SR, (t + 2) % T
                    dve.wait_ge(exp_done, n + 3)
                    dve.reciprocal(inv_sum[:, k:k + 1], row_sum[:, k:k + 1])
                    if isinstance(b, int) and n == -2:
                        dve.wait_ge(beta_done, 1)
                    dve.scalar_tensor_tensor(out=score[:, k % ZR, m * P:(m + 1) * P], in0=beta_ident[:, :],
                                             scalar=row_sum[:, k:k + 1], in1=score[:, k % ZR, m * P:(m + 1) * P],
                                             op0=ALU.mult, op1=ALU.add).then_inc(prob_ready, 1)
                if out_pair:
                    for i in range(2):
                        last = dve.bn_aggr(o_mv[:, i, :], o_stats[:, i, :])
                    last.then_inc(omv_done, 1)
                    dve.wait_ge(omv_done, b * PAIRS - PAIRS + t - 3)
                    dve.tensor_scalar(o_var_eps[:, :], o_mv[:, :, 1], EPS, None, ALU.add).then_inc(ove_done, 1)
                if live(b, t):
                    k = t % SR
                    dve.wait_ge(r_done, n + 1)
                    dve.bn_stats(stats[:, k, :], x1[:, slot(u, t), :]).then_inc(stats_done, 1)
                if out_pair:
                    dve.wait_ge(orstd_done, b * PAIRS - PAIRS + t - 3)
                    for i in range(2):
                        s = slot(1 - u, 2 * (t - 4) + i)
                        last = dve.tensor_scalar(x1[:, s, :], x1[:, s, :], o_mv[:, i, 0:1], o_rstd[:, i:i + 1],
                                                 ALU.subtract, ALU.mult)
                    last.then_inc(result_ready, 1)
                if batch_live(b - 1) and t == 2:
                    residual(b - 1, 1 - u, 0)
                k = adjT_step(b, t)
                if k is not None:
                    dve.wait_ge(adjT_rounded, k + 1)
                    dve.tensor_tensor(adjT_lo[:, k, :], adjT_raw[k % 2], adjT_hi[:, k, :].bitcast(F32),
                                      ALU.subtract).then_inc(adjT_split, 1)
                if isinstance(b, int) and b == -1:
                    dve.wait_ge(adj_in[t], 16)
                    dve.reduce_sum(deg[:, t:t + 1], adj_sb[:, t, :], AXX).then_inc(deg_done, 1)
                if isinstance(b, int) and b == -1 and t == T - 1:
                    dve.wait_ge(deg_done, T)
                    dve.tensor_scalar(deg_pos[:, :], deg[:, :], 0.0, None, ALU.is_gt)
                    dve.tensor_scalar(deg[:, :], deg[:, :], TINY, None, ALU.max).then_inc(deg_clamped, 1)
                if isinstance(b, int) and b == 0 and t == 0:
                    dve.wait_ge(deg_rooted, 1)
                    dve.tensor_tensor(dis[:, :], dis[:, :], deg_pos[:, :], ALU.mult).then_inc(dis_ready, 1)

            steps(dve, step)

        @block.tensor
        def _(pe):
            def product(bank, lhs, rhs, pieces, first=True, last=True):
                passes = [(l, r, p) for p in pieces for l, r in ((0, 0), (0, 1), (1, 0))]
                for j, (l, r, p) in enumerate(passes):
                    mm = pe.matmul(bank, lhs[l](p), rhs[r](p), start=first and j == 0,
                                   stop=last and j == len(passes) - 1)
                return mm

            def mix_taken_before(b, u, t):
                n = b * T + t
                if batch_live(b + 1) and 1 <= t <= 4:
                    pe.wait_ge(h_split, b * T + T + 2 * t)
                elif batch_live(b + 1) and t == 5:
                    pe.wait_ge(s2b_ready, b * 2 + 4)
                elif live(b, t, -3):
                    pe.wait_ge(sup_split, n - 2)

            def make_h(b, par, j):
                q = j // 2
                if j % 2 == 0:
                    pe.wait_ge(x_split, b * PAIRS + q + 1)
                    if isinstance(b, int) and b == 0 and j == 0:
                        pe.wait_ge(w_split, 2)
                cols = slice((j % 2) * P, (j % 2 + 1) * P)
                product(bank_mix[:, 0:HC],
                        [lambda c, s=s: s[:, q % 2, c, cols] for s in (xs_hi, xs_lo)],
                        [lambda c, w=w: w[:, c, :] for w in (w0_hi, w0_lo)], range(C)).then_inc(h_done, 1)

            def s2_rows(b, par, i):
                if i == 0:
                    pe.wait_ge(s_ready, b + 1)
                for j in range(4):
                    mm = pe.transpose(bank_mix[:, j * P:(j + 1) * P],
                                      s12[:, par, 4 * i + j, 1:2].to_broadcast([P, P]), ident[:, :])
                mm.then_inc(s2row_done, 1)

            def attend(u, i):
                return product(bank_att[:, 0:D], [lambda k, p=p: p[:, k, :] for p in (pt_hi, pt_lo)],
                               [lambda k, h=h: h[:, u, k, 0:D] for h in (h_hi, h_lo)],
                               range(4 * i, 4 * i + 4), first=i == 0, last=i == 1)

            def accumulate(par, k, i):
                for j in range(4 * i, 4 * i + 4):
                    for p, (l, r) in enumerate(((adjT_hi, sup_hi), (adjT_hi, sup_lo), (adjT_lo, sup_hi))):
                        mm = pe.matmul(bank_acc[j // 2][:, (j % 2) * D:(j % 2 + 1) * D],
                                       l[:, k, j * P:(j + 1) * P], r[:, par, :],
                                       start=k == 0 and j % 2 == 0 and p == 0,
                                       stop=k == T - 1 and p == 2, skip_group_check=True)
                if k == T - 1:
                    mm.then_inc(acc_done, 1)

            pe.wait_ge(const_done, 2)

            def step(b, half, u, t):
                n = b * T + t
                if live(b, t, -2):
                    mix_taken_before(b, u, t)
                    pe.wait_ge(x1_ready, n - 1)
                    s = slot(u, t, -2)
                    for c in range(C):
                        mm = pe.transpose(bank_mix[:, c * P:(c + 1) * P], x1[:, s, c * P:(c + 1) * P], ident[:, :])
                    mm.then_inc(x1t_done, 1)
                if live(b, t):
                    if t == 0:
                        pe.wait_ge(h_split, b * T + T)
                    wait(pe, elu_done, n)
                    pe.wait_ge(pt_split, n * 2 + 1)
                    attend(u, 0)
                if batch_live(b + 1) and t <= 4:
                    if live(b, t, -2):
                        pe.wait_ge(x1t_split, n - 1)
                    else:
                        mix_taken_before(b, u, t)
                    if t < 4:
                        make_h(b + 1, 1 - u, 2 * t)
                    else:
                        s2_rows(b + 1, 1 - u, 0)
                if live(b, t):
                    pe.wait_ge(pt_split, n * 2 + 2)
                    attend(u, 1).then_inc(att_done, 1)
                if batch_live(b + 1) and t <= 4:
                    if t < 4:
                        pe.wait_ge(h_split, b * T + T + 2 * t + 1)
                    else:
                        pe.wait_ge(s2b_ready, b * 2 + 3)
                if live(b, t, -2):
                    if isinstance(b, int) and n == 2:
                        pe.wait_ge(w_split, 3)
                    pe.wait_ge(x1t_split, n - 1)
                    product(bank_mix[:, 0:D],
                            [lambda c, s=s: s[:, c * P:(c + 1) * P] for s in (x1t_hi, x1t_lo)],
                            [lambda c, w=w: w[:, c, :] for w in (w1_hi, w1_lo)], range(C)).then_inc(sup_done, 1)
                if live(b, t, 1):
                    pe.wait_ge(prob_ready, n + 2)
                    for i in range(2):
                        for j in range(4):
                            k = 4 * i + j
                            mm = pe.transpose(bank_pt[i][:, j * P:(j + 1) * P],
                                              score[:, (t + 1) % ZR, k * P:(k + 1) * P], ident[:, :])
                        mm.then_inc(pt_done, 1)
                k = (t - 3) % T
                if live(b, t, -3):
                    if isinstance(b, int) and n - 3 < T:
                        pe.wait_ge(adjT_split, k + 1)
                    if k == 0:
                        wait(pe, r2_done, b * T - T + 4)
                    pe.wait_ge(sup_split, n - 2)
                    accumulate((t - 1) % 2, k, 0)
                if batch_live(b + 1) and t <= 4:
                    if live(b, t, -2):
                        pe.wait_ge(sup_split, n - 1)
                    if t < 4:
                        make_h(b + 1, 1 - u, 2 * t + 1)
                    else:
                        s2_rows(b + 1, 1 - u, 1)
                if live(b, t, -3):
                    if k == 0:
                        wait(pe, r2_done, b * T - T + 8)
                    accumulate((t - 1) % 2, k, 1)

            steps(pe, step)


def kernel(x, adj, L0_gnn_W, L0_gnn_a, L0_gnn_beta, L1_gnn_weight, L1_gnn_bias):
    import numpy as np
    import concourse.bacc as bacc
    from concourse.bass_utils import run_bass_kernel_spmd

    x = np.asarray(x)
    adj = np.asarray(adj)
    pairs = B * PAIRS
    arrays = {
        "x_d": x.reshape(pairs, 2, P, D).transpose(0, 2, 1, 3),
        "xT_d": x.reshape(pairs, 2 * P, C, P).transpose(0, 3, 2, 1),
        "adj_d": adj.reshape(T, P, N),
        "adjT_d": adj.T.reshape(T, P, N),
        "W0_d": np.asarray(L0_gnn_W).reshape(C, P, D).transpose(1, 0, 2),
        "a_d": np.asarray(L0_gnn_a).reshape(1, 2 * D),
        "beta_d": np.asarray(L0_gnn_beta).reshape(1, 1),
        "W1_d": np.asarray(L1_gnn_weight).reshape(C, P, D).transpose(1, 0, 2),
        "bias_d": np.asarray(L1_gnn_bias).reshape(1, D),
    }
    arrays = {name: np.ascontiguousarray(v) for name, v in arrays.items()}
    nc = bacc.Bacc("TRN2", target_bir_lowering=False, num_devices=1)
    args = [nc.dram_tensor(name, v.shape, mybir.dt.from_np(v.dtype), kind="ExternalInput").ap()
            for name, v in arrays.items()]
    out = nc.dram_tensor("out_d", (pairs, P, 2, D), F32, kind="ExternalOutput").ap()
    build(nc, *args, out)
    result = run_bass_kernel_spmd(nc, [arrays], core_ids=[0]).results[0]["out_d"]
    return np.ascontiguousarray(result.transpose(0, 2, 1, 3)).reshape(B, N, D)
```

```python
from contextlib import ExitStack

import concourse.bass as bass
import concourse.mybir as mybir

F32 = mybir.dt.float32
F32R = mybir.dt.float32r
ALU = mybir.AluOpType
ACT = mybir.ActivationFunctionType
AXX = mybir.AxisListType.X

P = 128
B, N, D = 8, 1024, 256
T = N // P
C = D // P
NT = B * T
HC = D + 2
PAIRS = T // 2
HALF = T // 2 * P
SLOPE = 0.2
EPS = 1e-5
TINY = 1.2e-38
ZR = 4
SR = 4
XS = 2 * T


def build(nc, x, xT, adj, adjT, W0, a, beta, W1, bias, out):
    with ExitStack() as ctx:
        def sb(name, shape, dt=F32):
            return ctx.enter_context(nc.sbuf_tensor(name, shape, dt))

        def pb(name):
            return ctx.enter_context(nc.psum_tensor(name, [P, 512], F32))

        def sem(name):
            return ctx.enter_context(nc.semaphore(name))

        adj_sb = sb("adj_sb", [P, T, N])
        adjT_hi = sb("adjT_hi", [P, T, N], F32R)
        adjT_lo = sb("adjT_lo", [P, T, N], F32R)
        w0_hi = sb("w0_hi", [P, C, HC], F32R)
        w0_lo = sb("w0_lo", [P, C, HC], F32R)
        w1_hi = sb("w1_hi", [P, C, D], F32R)
        w1_lo = sb("w1_lo", [P, C, D], F32R)
        ident = sb("ident", [P, P])
        beta_ident = sb("beta_ident", [P, P])
        bias_bc = sb("bias_bc", [P, D])
        beta_bc = sb("beta_bc", [P, 1])
        deg = sb("deg", [P, T])
        deg_pos = sb("deg_pos", [P, T])
        dis = sb("dis", [P, T])
        neg_half = sb("neg_half", [P, T])
        neg_one = sb("neg_one", [P, 2])
        xT_sb = sb("xT_sb", [P, 2, C, 2 * P])
        xs_hi = sb("xs_hi", [P, 2, C, 2 * P], F32R)
        xs_lo = sb("xs_lo", [P, 2, C, 2 * P], F32R)
        h_hi = sb("h_hi", [P, 2, T, HC], F32R)
        h_lo = sb("h_lo", [P, 2, T, HC], F32R)
        s12 = sb("s12", [P, 2, T, 2])
        s2b = sb("s2b", [P, N])
        score = sb("score", [P, ZR, N])
        row_max = sb("row_max", [P, SR])
        neg_max = sb("neg_max", [P, SR])
        row_sum = sb("row_sum", [P, SR])
        inv_sum = sb("inv_sum", [P, SR])
        pt_hi = sb("pt_hi", [P, T, P], F32R)
        pt_lo = sb("pt_lo", [P, T, P], F32R)
        whole = sb("whole", [P, 2, HC])
        elu = sb("elu", [P, 2, D])
        stats = sb("stats", [P, SR, 6])
        mv = sb("mv", [P, SR, 2])
        var_eps = sb("var_eps", [P, SR])
        rstd = sb("rstd", [P, SR])
        mean_rstd = sb("mean_rstd", [P, SR])
        shift = sb("shift", [P, SR])
        x1 = sb("x1", [P, XS, D])
        x1t_hi = sb("x1t_hi", [P, C * P], F32R)
        x1t_lo = sb("x1t_lo", [P, C * P], F32R)
        sup_hi = sb("sup_hi", [P, 2, D], F32R)
        sup_lo = sb("sup_lo", [P, 2, D], F32R)
        o_stats = sb("o_stats", [P, 2, 6])
        o_mv = sb("o_mv", [P, 2, 2])
        o_var_eps = sb("o_var_eps", [P, 2])
        o_rstd = sb("o_rstd", [P, 2])
        o_mean_rstd = sb("o_mean_rstd", [P, 2])
        o_shift = sb("o_shift", [P, 2])
        v12 = sb("v12", [P, C, 2])
        w0_raw = score[:, 3, 0:C * D].rearrange("p (c d) -> p c d", c=C)
        a_bc = score[:, 3, C * D:C * D + 2 * D]
        w1_raw = score[:, 2, 0:C * D].rearrange("p (c d) -> p c d", c=C)
        products = score[:, 1, :].rearrange("p (v d) -> p v d", v=2 * C)
        adjT_raw = [x1[:, T + 4 * k:T + 4 * k + 4, :].rearrange("p s d -> p (s d)") for k in range(2)]

        bank_pt = [pb("bank_pt0"), pb("bank_pt1")]
        bank_att = pb("bank_att")
        bank_mix = pb("bank_mix")
        bank_acc = [pb(f"bank_acc{i}") for i in range(4)]
        bank_h0 = [bank_mix, bank_att, *bank_acc, *bank_pt]

        x_in = [sem(f"x_in{s}") for s in range(XS // 2)]
        out_done = [sem(f"out_done{s}") for s in range(XS // 2)]
        xT_in = [sem(f"xT_in{q}") for q in range(2)]
        adj_in = [sem(f"adj_in{t}") for t in range(T)]
        adjT_in = [sem(f"adjT_in{k}") for k in range(2)]
        w0_in, w1_in, bias_in, beta_in, a_in = (
            sem("w0_in"), sem("w1_in"), sem("bias_in"), sem("beta_in"), sem("a_in"))
        const_done = sem("const_done")
        v_done, w0_rounded, w1_rounded, w_split = sem("v_done"), sem("w0_rounded"), sem("w1_rounded"), sem("w_split")
        beta_done = sem("beta_done")
        adjT_rounded, adjT_split = sem("adjT_rounded"), sem("adjT_split")
        deg_done, deg_clamped, deg_rooted, dis_ready = (
            sem("deg_done"), sem("deg_clamped"), sem("deg_rooted"), sem("dis_ready"))
        x_rounded, x_split = sem("x_rounded"), sem("x_split")
        h_done, h_rounded, h_split = sem("h_done"), sem("h_rounded"), sem("h_split")
        s_ready, s2row_done, s2b_ready = sem("s_ready"), sem("s2row_done"), sem("s2b_ready")
        z_ready, leaky_done, max_done, negmax_done = (
            sem("z_ready"), sem("leaky_done"), sem("max_done"), sem("negmax_done"))
        exp_done, prob_ready = sem("exp_done"), sem("prob_ready")
        pt_done, pt_rounded, pt_split = sem("pt_done"), sem("pt_rounded"), sem("pt_split")
        att_done, eu_done, em_done, elu_done = sem("att_done"), sem("eu_done"), sem("em_done"), sem("elu_done")
        r_done, stats_done, mv_done, ve_done = sem("r_done"), sem("stats_done"), sem("mv_done"), sem("ve_done")
        rstd_done, x1_ready, x1b_done = sem("rstd_done"), sem("x1_ready"), sem("x1b_done")
        mean_rstd_done, shift_done = sem("mean_rstd_done"), sem("shift_done")
        omean_rstd_done, oshift_done = sem("omean_rstd_done"), sem("oshift_done")
        x1t_done, x1t_rounded, x1t_split = sem("x1t_done"), sem("x1t_rounded"), sem("x1t_split")
        sup_done, sup_rounded, sup_split = sem("sup_done"), sem("sup_rounded"), sem("sup_split")
        acc_done, r2_done, ostats_done, omv_done, ove_done, orstd_done, result_ready = (
            sem("acc_done"), sem("r2_done"), sem("ostats_done"), sem("omv_done"), sem("ove_done"),
            sem("orstd_done"), sem("result_ready"))

        def wait(eng, signal, count):
            if not isinstance(count, int) or count > 0:
                eng.wait_ge(signal, count)

        def live(b, t, shift=0):
            return not isinstance(b, int) or 0 <= T * b + t + shift < NT

        def batch_live(b):
            return not isinstance(b, int) or 0 <= b < B

        def steps(eng, step):
            for g in range(-T // 2, T):
                step(g // T, g // T // 2, g // T % 2, g % T)
            with eng.Fori(0, (B - 2) // 2) as i:
                for b, half, u in ((i * 2 + 1, i, 1), (i * 2 + 2, i + 1, 0)):
                    for t in range(T):
                        step(b, half, u, t)
            for b in (B - 1, B):
                for t in range(T):
                    step(b, b // 2, b % 2, t)

        def deg_group(b, t):
            return {-1: 0, 2: 1}.get(T * b + t) if isinstance(b, int) else None

        def slot(u, t, shift=0):
            return (T * u + t + shift) % XS

        def adjT_step(b, t):
            k = T * b + t + 1 if isinstance(b, int) else -1
            return k if 0 <= k < T else None

        def deg_steps(b, t):
            g = T * b + t if isinstance(b, int) else T
            return (0, 1) if g == -T // 2 else (g + T // 2 + 1,) if -T // 2 < g < T // 2 - 1 else ()

        block = ctx.enter_context(nc.Block())

        @block.sync
        def _(sp):
            def load_xT(b, q):
                m = b * PAIRS + q
                wait(sp, x_split, m - 1)
                sp.dma_start(xT_sb[:, q % 2, :, :], xT[m]).then_inc(xT_in[q % 2], 16)

            def load_x(b, u, q):
                s = slot(u, 2 * q)
                sp.dma_start(x1[:, s:s + 2, :], x[b * PAIRS + q]).then_inc(x_in[s // 2], 16)

            def round_(b, half_before, u):
                for c, q in ((b + 1, 2), (b + 1, 3), (b + 2, 0), (b + 2, 1)):
                    if batch_live(c):
                        load_xT(c, q)
                for q in range(PAIRS):
                    s = slot(1 - u, 2 * q)
                    if batch_live(b - 1):
                        sp.wait_ge(result_ready, (b - 1) * PAIRS + q + 1)
                        sp.dma_start(out[(b - 1) * PAIRS + q], x1[:, s:s + 2, :]).then_inc(out_done[s // 2], 16)
                for q in range(PAIRS):
                    s = slot(1 - u, 2 * q)
                    if batch_live(b - 1) and batch_live(b + 1):
                        sp.wait_ge(out_done[s // 2], (half_before + 1) * 16)
                        load_x(b + 1, 1 - u, q)

            load_xT(0, 0)
            sp.dma_start(w0_raw, W0).then_inc(w0_in, 16)
            sp.dma_start(a_bc, a.to_broadcast([P, 2 * D])).then_inc(a_in, 16)
            load_xT(0, 1)
            sp.dma_start(beta_bc[:, :], beta.to_broadcast([P, 1])).then_inc(beta_in, 16)
            sp.dma_start(w1_raw, W1).then_inc(w1_in, 16)
            sp.dma_start(bias_bc[:, :], bias.to_broadcast([P, D])).then_inc(bias_in, 16)
            for t in range(1):
                sp.dma_start(adj_sb[:, t, :], adj[t]).then_inc(adj_in[t], 16)
            load_xT(0, 2)
            load_xT(0, 3)
            for t in range(1, T):
                sp.dma_start(adj_sb[:, t, :], adj[t]).then_inc(adj_in[t], 16)
            for k in range(2):
                sp.dma_start(adjT_raw[k], adjT[k]).then_inc(adjT_in[k], 16)
            load_x(0, 0, 0)
            load_xT(1, 0)
            load_xT(1, 1)
            for q in range(1, PAIRS):
                load_x(0, 0, q)
            for k in range(2, T):
                if k in (3, 4):
                    load_xT(1, k - 1)
                sp.wait_ge(adjT_split, k - 1)
                sp.dma_start(adjT_raw[k % 2], adjT[k]).then_inc(adjT_in[k % 2], 16)
            sp.wait_ge(adjT_split, T)
            for q in range(PAIRS):
                load_x(1, 1, q)
            load_xT(2, 0)
            load_xT(2, 1)
            with sp.Fori(0, (B - 4) // 2) as i:
                round_(i * 2 + 1, i, 1)
                round_(i * 2 + 2, i, 0)
            for b in range(B - 3, B + 1):
                round_(b, (b - 1) // 2, b % 2)
            for s in range(XS // 2):
                sp.wait_ge(out_done[s], 16 * (B // 2))

        @block.gpsimd
        def _(pool):
            pool.memset(neg_half[:, :], -0.5)
            pool.memset(neg_one[:, :], -1.0)
            pool.memset(ident[:, :], 0.0).then_inc(const_done, 1)
            pool.wait_ge(const_done, 1)
            pool.affine_select(out=ident[:, :], in_=ident[:, :], compare_op=ALU.not_equal, fill=1.0, base=0,
                               pattern=[[-1, P]], channel_multiplier=1).then_inc(const_done, 1)
            pool.wait_ge(const_done, 2)

            def rest_of_h(b, par, j):
                pool.wait_ge(h_rounded, b * T + j + 1)
                pool.tensor_tensor(h_lo[:, par, j, :], whole[:, 1, :], h_hi[:, par, j, :].bitcast(F32),
                                   ALU.subtract).then_inc(h_split, 1)

            def step(b, half, u, t):
                n = b * T + t
                if live(b, t, -2):
                    pool.wait_ge(x1t_rounded, n - 1)
                    pool.tensor_tensor(x1t_lo[:, :], whole[:, 0, 0:D], x1t_hi[:, :].bitcast(F32),
                                       ALU.subtract).then_inc(x1t_split, 1)
                if batch_live(b - 1) and t >= 4:
                    m = (b - 1) * PAIRS + t - 3
                    wait(pool, result_ready, m - 1)
                    pool.wait_ge(ove_done, m)
                    pool.tensor_tensor(o_rstd[:, :], o_var_eps[:, :], neg_half[:, 0:2], ALU.pow).then_inc(orstd_done, 1)
                    pool.wait_ge(orstd_done, m)
                    pool.tensor_tensor(o_mean_rstd[:, :], o_mv[:, :, 0], o_rstd[:, :],
                                       ALU.mult).then_inc(omean_rstd_done, 1)
                    pool.wait_ge(omean_rstd_done, m)
                    pool.tensor_tensor(o_shift[:, :], o_mean_rstd[:, :], neg_one[:, :], ALU.mult).then_inc(oshift_done, 1)
                if live(b, t, -1):
                    k = (t - 1) % SR
                    one = slice(k, k + 1)
                    pool.wait_ge(ve_done, n)
                    pool.tensor_tensor(rstd[:, one], var_eps[:, one], neg_half[:, 0:1], ALU.pow).then_inc(rstd_done, 1)
                    pool.wait_ge(rstd_done, n)
                    pool.tensor_tensor(mean_rstd[:, one], mv[:, k, 0:1], rstd[:, one],
                                       ALU.mult).then_inc(mean_rstd_done, 1)
                    pool.wait_ge(mean_rstd_done, n)
                    pool.tensor_tensor(shift[:, one], mean_rstd[:, one], neg_one[:, 0:1],
                                       ALU.mult).then_inc(shift_done, 1)
                if batch_live(b + 1) and t < 4:
                    rest_of_h(b + 1, 1 - u, 2 * t)
                if live(b, t, -2):
                    s = slot(u, t, -2)
                    pool.wait_ge(sup_rounded, n - 1)
                    pool.tensor_tensor(sup_lo[:, t % 2, :], whole[:, 0, 0:D], sup_hi[:, t % 2, :].bitcast(F32),
                                       ALU.subtract).then_inc(sup_split, 1)
                    if isinstance(b, int) and n == 2:
                        pool.wait_ge(bias_in, 16)
                    pool.tensor_tensor(x1[:, s, :], x1[:, s, :], bias_bc[:, :], ALU.add).then_inc(x1b_done, 1)
                if live(b, t):
                    s = slot(u, t)
                    pool.wait_ge(x_in[s // 2], (half + 1) * 16)
                    pool.wait_ge(elu_done, n + 1)
                    pool.tensor_tensor(x1[:, s, :], x1[:, s, :], elu[:, t % 2, :], ALU.add).then_inc(r_done, 1)
                if batch_live(b + 1) and t < 4:
                    rest_of_h(b + 1, 1 - u, 2 * t + 1)
                i = deg_group(b, t)
                if i is not None:
                    cols = slice(4 * i, 4 * i + 4)
                    pool.wait_ge(deg_clamped, i + 1)
                    pool.tensor_tensor(dis[:, cols], deg[:, cols], neg_half[:, cols], ALU.pow).then_inc(deg_rooted, 1)

            steps(pool, step)

        @block.scalar
        def _(act):
            act.wait_ge(w0_in, 16)
            nc.scalar.activation(w0_hi[:, :, 0:D], w0_raw, ACT.Copy).then_inc(w0_rounded, 1)
            act.wait_ge(v_done, 1)
            nc.scalar.activation(w0_hi[:, :, D:HC], v12[:, :, :], ACT.Copy).then_inc(w0_rounded, 1)

            def round_h(b, par, j):
                act.wait_ge(h_done, b * T + j + 1)
                nc.scalar.activation(h_hi[:, par, j, :], bank_mix[:, 0:HC], ACT.Copy)
                wait(act, h_split, b * T + j)
                nc.scalar.activation(whole[:, 1, :], bank_mix[:, 0:HC], ACT.Copy).then_inc(h_rounded, 1)

            def normalize_out(b, u, q):
                act.wait_ge(oshift_done, b * PAIRS + q + 1)
                for i in range(2):
                    s = slot(u, 2 * q + i)
                    last = nc.scalar.activation(x1[:, s, :], x1[:, s, :], ACT.Identity,
                                                scale=o_rstd[:, i:i + 1], bias=o_shift[:, i:i + 1])
                last.then_inc(result_ready, 1)

            def copy_s2(b, i):
                if i == 0:
                    wait(act, z_ready, b * T)
                act.wait_ge(s2row_done, b * 2 + i + 1)
                nc.scalar.activation(s2b[:, i * HALF:(i + 1) * HALF], bank_mix[:, :], ACT.Copy).then_inc(s2b_ready, 1)

            for j in range(T):
                act.wait_ge(h_done, j + 1)
                nc.scalar.activation(h_hi[:, 0, j, :], bank_h0[j][:, 0:HC], ACT.Copy).then_inc(h_rounded, 1)
            act.wait_ge(w1_in, 16)
            nc.scalar.activation(w1_hi[:, :, :], w1_raw, ACT.Copy).then_inc(w1_rounded, 1)

            def step(b, half, u, t):
                n = b * T + t
                if live(b, t, -2):
                    act.wait_ge(x1t_done, n - 1)
                    nc.scalar.activation(x1t_hi[:, :], bank_mix[:, 0:D], ACT.Copy)
                    wait(act, sup_split, n - 2)
                    nc.scalar.activation(whole[:, 0, 0:D], bank_mix[:, 0:D], ACT.Copy).then_inc(x1t_rounded, 1)
                if live(b, t, 3):
                    tz = (t + 3) % T
                    par = u if t + 3 < T else 1 - u
                    if tz == 0:
                        act.wait_ge(s2b_ready, b * 2 + 4)
                    if isinstance(b, int) and n in (-1, 0):
                        act.wait_ge(w_split, 3)
                    wait(act, pt_done, n * 2)
                    nc.scalar.activation(score[:, (t + 3) % ZR, :], s2b[:, :], ACT.Identity,
                                         bias=s12[:, par, tz, 0:1]).then_inc(z_ready, 1)
                if batch_live(b + 1) and t < 4:
                    round_h(b + 1, 1 - u, 2 * t)
                if batch_live(b + 1) and t == 4:
                    copy_s2(b + 1, 0)
                if live(b, t):
                    act.wait_ge(att_done, n + 1)
                    wait(act, r_done, n - 1)
                    nc.scalar.activation(elu[:, t % 2, :], bank_att[:, 0:D], ACT.Exp,
                                         scale=inv_sum[:, t % SR:t % SR + 1]).then_inc(eu_done, 1)
                if live(b, t, -2):
                    k = (t - 2) % T
                    act.wait_ge(sup_done, n - 1)
                    if isinstance(b, int) and n in (2, 6):
                        act.wait_ge(dis_ready, n // 4 + 1)
                    nc.scalar.activation(sup_hi[:, t % 2, :], bank_mix[:, 0:D], ACT.Copy, scale=dis[:, k:k + 1])
                    nc.scalar.activation(whole[:, 0, 0:D], bank_mix[:, 0:D], ACT.Copy,
                                         scale=dis[:, k:k + 1]).then_inc(sup_rounded, 1)
                if live(b, t, 1):
                    for i in range(2):
                        act.wait_ge(pt_done, n * 2 + 3 + i)
                        nc.scalar.activation(pt_hi[:, 4 * i:4 * i + 4, :], bank_pt[i][:, :].rearrange(
                            "p (k q) -> p k q", k=4), ACT.Copy).then_inc(pt_rounded, 1)
                if live(b, t, -1):
                    k, s = (t - 1) % SR, slot(u, t, -1)
                    act.wait_ge(shift_done, n)
                    nc.scalar.activation(x1[:, s, :], x1[:, s, :], ACT.Identity, scale=rstd[:, k:k + 1],
                                         bias=shift[:, k:k + 1]).then_inc(x1_ready, 1)
                if batch_live(b - 1) and t >= 4:
                    normalize_out(b - 1, 1 - u, t - 4)
                if batch_live(b + 1) and t < 4:
                    round_h(b + 1, 1 - u, 2 * t + 1)
                if batch_live(b + 1) and t == 4:
                    copy_s2(b + 1, 1)
                if live(b, t, 2):
                    k = (t + 2) % SR
                    act.wait_ge(negmax_done, n + 3)
                    nc.scalar.activation(score[:, k % ZR, :], score[:, k % ZR, :], ACT.Exp,
                                         bias=neg_max[:, k:k + 1],
                                         accum_out=row_sum[:, k:k + 1]).then_inc(exp_done, 1)
                k = adjT_step(b, t)
                if k is not None:
                    act.wait_ge(adjT_in[k % 2], 16 * (k // 2 + 1))
                    nc.scalar.activation(adjT_hi[:, k, :], adjT_raw[k % 2], ACT.Copy).then_inc(adjT_rounded, 1)

            steps(act, step)

        @block.vector
        def _(dve):
            dve.memset(row_max[:, :], 0.0)
            dve.wait_ge(w0_in, 16)
            dve.wait_ge(a_in, 16)
            for c in range(C):
                for j in range(2):
                    last = dve.tensor_tensor_reduce(out=products[:, 2 * c + j, :], in0=w0_raw[:, c, :], in1=a_bc[:, j * D:(j + 1) * D],
                                                    scale=1.0, scalar=0.0, op0=ALU.mult, op1=ALU.add,
                                                    accum_out=v12[:, c, j:j + 1])
            last.then_inc(v_done, 1)
            dve.wait_ge(w0_rounded, 1)
            dve.tensor_tensor(w0_lo[:, :, 0:D], w0_raw, w0_hi[:, :, 0:D].bitcast(F32), ALU.subtract).then_inc(w_split, 1)
            dve.wait_ge(w0_rounded, 2)
            dve.tensor_tensor(w0_lo[:, :, D:HC], v12[:, :, :], w0_hi[:, :, D:HC].bitcast(F32),
                              ALU.subtract).then_inc(w_split, 1)

            def split_x(b, q):
                m = b * PAIRS + q
                dve.wait_ge(xT_in[q % 2], (b * 2 + q // 2 + 1) * 16)
                wait(dve, h_done, (m - 1) * 2)
                dve.tensor_copy(xs_hi[:, q % 2, :, :], xT_sb[:, q % 2, :, :]).then_inc(x_rounded, 1)
                dve.wait_ge(x_rounded, m + 1)
                dve.tensor_tensor(xs_lo[:, q % 2, :, :], xT_sb[:, q % 2, :, :],
                                  xs_hi[:, q % 2, :, :].bitcast(F32), ALU.subtract).then_inc(x_split, 1)

            def rests_of_h0(q):
                for j in (2 * q, 2 * q + 1):
                    dve.wait_ge(h_rounded, j + 1)
                    dve.tensor_tensor(h_lo[:, 0, j, :], bank_h0[j][:, 0:HC], h_hi[:, 0, j, :].bitcast(F32),
                                      ALU.subtract).then_inc(h_split, 1)

            def sum_s(b, par):
                dve.wait_ge(h_split, b * T + T)
                dve.tensor_tensor(s12[:, par, :, :], h_hi[:, par, :, D:HC].bitcast(F32),
                                  h_lo[:, par, :, D:HC].bitcast(F32), ALU.add).then_inc(s_ready, 1)

            def residual(b, u, i):
                dve.wait_ge(x1b_done, b * T + T)
                dve.wait_ge(acc_done, b * 2 + i + 1)
                for j in range(4 * i, 4 * i + 4):
                    s = slot(u, j)
                    dve.scalar_tensor_tensor(out=x1[:, s, :], in0=bank_acc[j // 2][:, (j % 2) * D:(j % 2 + 1) * D],
                                             scalar=dis[:, j:j + 1], in1=x1[:, s, :], op0=ALU.mult,
                                             op1=ALU.add).then_inc(r2_done, 1)

            def step(b, half, u, t):
                n = b * T + t
                out_pair = batch_live(b - 1) and 3 <= t < 7
                if batch_live(b + 1) and t == 0:
                    split_x(b + 1, 0)
                if out_pair:
                    for i in range(2):
                        s = slot(1 - u, 2 * (t - 3) + i)
                        dve.wait_ge(r2_done, b * T - T + 2 * (t - 3) + i + 1)
                        dve.bn_stats(o_stats[:, i, :], x1[:, s, :]).then_inc(ostats_done, 1)
                if batch_live(b - 1) and t == 3:
                    residual(b - 1, 1 - u, 1)
                if live(b, t, -1):
                    dve.wait_ge(stats_done, n)
                if live(b, t, 2):
                    k = (t + 2) % ZR
                    dve.wait_ge(z_ready, n + 3)
                    dve.scalar_tensor_tensor(out=score[:, k, :], in0=score[:, k, :], scalar=SLOPE,
                                             in1=score[:, k, :], op0=ALU.mult, op1=ALU.max).then_inc(leaky_done, 1)
                if live(b, t, -1):
                    k = (t - 1) % SR
                    dve.bn_aggr(mv[:, k, :], stats[:, k, :]).then_inc(mv_done, 1)
                    if live(b, t, 2):
                        dve.wait_ge(leaky_done, n + 3)
                    dve.wait_ge(mv_done, n)
                    dve.tensor_scalar(var_eps[:, k:k + 1], mv[:, k, 1:2], EPS, None, ALU.add).then_inc(ve_done, 1)
                if live(b, t, 2):
                    k = (t + 2) % SR
                    m = (t + 2) % T
                    if isinstance(b, int) and n + 2 < T:
                        dve.wait_ge(adj_in[m], 16)
                    if not live(b, t, -1):
                        dve.wait_ge(leaky_done, n + 3)
                    dve.tensor_tensor_reduce(out=score[:, k % ZR, :], in0=score[:, k % ZR, :], in1=adj_sb[:, m, :],
                                             scale=1.0, scalar=-3.4e38, op0=ALU.mult, op1=ALU.max,
                                             accum_out=row_max[:, k:k + 1]).then_inc(max_done, 1)
                if live(b, t):
                    dve.wait_ge(eu_done, n + 1)
                    dve.tensor_scalar(elu[:, t % 2, :], elu[:, t % 2, :], 1.0, -1.0,
                                      ALU.min, ALU.add).then_inc(em_done, 1)
                if live(b, t, 2):
                    k = (t + 2) % SR
                    dve.wait_ge(max_done, n + 3)
                    dve.tensor_scalar(neg_max[:, k:k + 1], row_max[:, k:k + 1], -1.0, None,
                                      ALU.mult).then_inc(negmax_done, 1)
                if live(b, t):
                    e = elu[:, t % 2, :]
                    dve.wait_ge(em_done, n + 1)
                    dve.scalar_tensor_tensor(out=e, in0=bank_att[:, 0:D], scalar=inv_sum[:, t % SR:t % SR + 1],
                                             in1=e, op0=ALU.mult, op1=ALU.max).then_inc(elu_done, 1)
                if live(b, t, 1):
                    for i in range(2):
                        dve.wait_ge(pt_rounded, n * 2 + 3 + i)
                        dve.tensor_tensor(pt_lo[:, 4 * i:4 * i + 4, :], bank_pt[i][:, :].rearrange(
                            "p (k q) -> p k q", k=4), pt_hi[:, 4 * i:4 * i + 4, :].bitcast(F32),
                            ALU.subtract).then_inc(pt_split, 1)
                if batch_live(b + 1) and t < 3:
                    split_x(b + 1, t + 1)
                if batch_live(b + 1) and t == 3:
                    sum_s(b + 1, 1 - u)
                if out_pair:
                    wait(dve, omean_rstd_done, b * PAIRS - PAIRS + t - 3)
                    dve.wait_ge(ostats_done, b * T - T + 2 * (t - 3) + 2)
                if live(b, t, 2):
                    k, m = (t + 2) % SR, (t + 2) % T
                    dve.wait_ge(exp_done, n + 3)
                    dve.reciprocal(inv_sum[:, k:k + 1], row_sum[:, k:k + 1])
                    if isinstance(b, int) and n == -2:
                        dve.wait_ge(beta_done, 1)
                    dve.scalar_tensor_tensor(out=score[:, k % ZR, m * P:(m + 1) * P], in0=beta_ident[:, :],
                                             scalar=row_sum[:, k:k + 1], in1=score[:, k % ZR, m * P:(m + 1) * P],
                                             op0=ALU.mult, op1=ALU.add).then_inc(prob_ready, 1)
                if out_pair:
                    for i in range(2):
                        dve.bn_aggr(o_mv[:, i, :], o_stats[:, i, :]).then_inc(omv_done, 1)
                    dve.wait_ge(omv_done, b * T - T + 2 * (t - 3) + 2)
                    dve.tensor_scalar(o_var_eps[:, :], o_mv[:, :, 1], EPS, None, ALU.add).then_inc(ove_done, 1)
                if live(b, t):
                    k = t % SR
                    dve.wait_ge(r_done, n + 1)
                    dve.bn_stats(stats[:, k, :], x1[:, slot(u, t), :]).then_inc(stats_done, 1)
                if batch_live(b - 1) and t == 2:
                    residual(b - 1, 1 - u, 0)
                k = adjT_step(b, t)
                if k is not None:
                    dve.wait_ge(adjT_rounded, k + 1)
                    dve.tensor_tensor(adjT_lo[:, k, :], adjT_raw[k % 2], adjT_hi[:, k, :].bitcast(F32),
                                      ALU.subtract).then_inc(adjT_split, 1)
                for m in deg_steps(b, t):
                    dve.wait_ge(adj_in[m], 16)
                    dve.reduce_sum(deg[:, m:m + 1], adj_sb[:, m, :], AXX).then_inc(deg_done, 1)
                i = deg_group(b, t)
                if i is not None:
                    cols = slice(4 * i, 4 * i + 4)
                    dve.wait_ge(deg_done, 4 * i + 4)
                    dve.tensor_scalar(deg_pos[:, cols], deg[:, cols], 0.0, None, ALU.is_gt)
                    dve.tensor_scalar(deg[:, cols], deg[:, cols], TINY, None, ALU.max).then_inc(deg_clamped, 1)
                i = deg_group(b, t - 1)
                if i is not None:
                    cols = slice(4 * i, 4 * i + 4)
                    dve.wait_ge(deg_rooted, i + 1)
                    dve.tensor_tensor(dis[:, cols], dis[:, cols], deg_pos[:, cols], ALU.mult).then_inc(dis_ready, 1)

            for q in range(PAIRS):
                split_x(0, q)
                if q:
                    rests_of_h0(q - 1)
            rests_of_h0(PAIRS - 1)
            sum_s(0, 0)
            dve.wait_ge(w1_rounded, 1)
            dve.tensor_tensor(w1_lo[:, :, :], w1_raw, w1_hi[:, :, :].bitcast(F32), ALU.subtract).then_inc(w_split, 1)
            dve.wait_ge(const_done, 2)
            dve.wait_ge(beta_in, 16)
            dve.tensor_scalar(beta_ident[:, :], ident[:, :], beta_bc[:, :], None, ALU.mult).then_inc(beta_done, 1)
            steps(dve, step)

        @block.tensor
        def _(pe):
            def product(bank, lhs, rhs, pieces, first=True, last=True):
                passes = [(l, r, p) for p in pieces for l, r in ((0, 0), (0, 1), (1, 0))]
                for j, (l, r, p) in enumerate(passes):
                    mm = pe.matmul(bank, lhs[l](p), rhs[r](p), start=first and j == 0,
                                   stop=last and j == len(passes) - 1)
                return mm

            def mix_taken_before(b, u, t):
                n = b * T + t
                if isinstance(b, int) and b < 0 and t <= 4:
                    pass
                elif batch_live(b + 1) and 1 <= t <= 4:
                    pe.wait_ge(h_rounded, b * T + T + 2 * t)
                elif batch_live(b + 1) and t == 5:
                    pe.wait_ge(s2b_ready, b * 2 + 4)
                elif live(b, t, -3):
                    pe.wait_ge(sup_rounded, n - 2)

            def make_h(b, bank, j):
                q = j // 2
                if j % 2 == 0:
                    pe.wait_ge(x_split, b * PAIRS + q + 1)
                    if isinstance(b, int) and b == 0 and j == 0:
                        pe.wait_ge(w_split, 2)
                cols = slice((j % 2) * P, (j % 2 + 1) * P)
                product(bank[:, 0:HC],
                        [lambda c, s=s: s[:, q % 2, c, cols] for s in (xs_hi, xs_lo)],
                        [lambda c, w=w: w[:, c, :] for w in (w0_hi, w0_lo)], range(C)).then_inc(h_done, 1)

            def s2_rows(b, par, i):
                if i == 0:
                    pe.wait_ge(s_ready, b + 1)
                for j in range(4):
                    mm = pe.transpose(bank_mix[:, j * P:(j + 1) * P],
                                      s12[:, par, 4 * i + j, 1:2].to_broadcast([P, P]), ident[:, :])
                mm.then_inc(s2row_done, 1)

            def attend(u, i):
                return product(bank_att[:, 0:D], [lambda k, p=p: p[:, k, :] for p in (pt_hi, pt_lo)],
                               [lambda k, h=h: h[:, u, k, 0:D] for h in (h_hi, h_lo)],
                               range(4 * i, 4 * i + 4), first=i == 0, last=i == 1)

            def accumulate(par, k, i):
                for j in range(4 * i, 4 * i + 4):
                    for p, (l, r) in enumerate(((adjT_hi, sup_hi), (adjT_hi, sup_lo), (adjT_lo, sup_hi))):
                        mm = pe.matmul(bank_acc[j // 2][:, (j % 2) * D:(j % 2 + 1) * D],
                                       l[:, k, j * P:(j + 1) * P], r[:, par, :],
                                       start=k == 0 and j % 2 == 0 and p == 0,
                                       stop=k == T - 1 and p == 2, skip_group_check=True)
                if k == T - 1:
                    mm.then_inc(acc_done, 1)

            for j in range(T):
                make_h(0, bank_h0[j], j)
            pe.wait_ge(const_done, 2)

            def step(b, half, u, t):
                n = b * T + t
                if live(b, t, -2):
                    mix_taken_before(b, u, t)
                    pe.wait_ge(x1_ready, n - 1)
                    s = slot(u, t, -2)
                    for c in range(C):
                        mm = pe.transpose(bank_mix[:, c * P:(c + 1) * P], x1[:, s, c * P:(c + 1) * P], ident[:, :])
                    mm.then_inc(x1t_done, 1)
                if live(b, t):
                    if t == 0:
                        pe.wait_ge(h_split, b * T + T)
                    wait(pe, elu_done, n)
                    pe.wait_ge(pt_split, n * 2 + 1)
                    attend(u, 0)
                if batch_live(b + 1) and t <= 4:
                    if live(b, t, -2):
                        pe.wait_ge(x1t_rounded, n - 1)
                    else:
                        mix_taken_before(b, u, t)
                    if t < 4:
                        make_h(b + 1, bank_mix, 2 * t)
                    else:
                        s2_rows(b + 1, 1 - u, 0)
                if live(b, t):
                    pe.wait_ge(pt_split, n * 2 + 2)
                    attend(u, 1).then_inc(att_done, 1)
                if batch_live(b + 1) and t <= 4:
                    if t < 4:
                        pe.wait_ge(h_rounded, b * T + T + 2 * t + 1)
                    else:
                        pe.wait_ge(s2b_ready, b * 2 + 3)
                if live(b, t, -2):
                    if isinstance(b, int) and n == 2:
                        pe.wait_ge(w_split, 3)
                    pe.wait_ge(x1t_split, n - 1)
                    product(bank_mix[:, 0:D],
                            [lambda c, s=s: s[:, c * P:(c + 1) * P] for s in (x1t_hi, x1t_lo)],
                            [lambda c, w=w: w[:, c, :] for w in (w1_hi, w1_lo)], range(C)).then_inc(sup_done, 1)
                if live(b, t, 1):
                    pe.wait_ge(prob_ready, n + 2)
                    for i in range(2):
                        for j in range(4):
                            k = 4 * i + j
                            mm = pe.transpose(bank_pt[i][:, j * P:(j + 1) * P],
                                              score[:, (t + 1) % ZR, k * P:(k + 1) * P], ident[:, :])
                        mm.then_inc(pt_done, 1)
                k = (t - 3) % T
                if live(b, t, -3):
                    if isinstance(b, int) and n - 3 < T:
                        pe.wait_ge(adjT_split, k + 1)
                    if k == 0:
                        wait(pe, r2_done, b * T - T + 4)
                    pe.wait_ge(sup_split, n - 2)
                    accumulate((t - 1) % 2, k, 0)
                if batch_live(b + 1) and t <= 4:
                    if live(b, t, -2):
                        pe.wait_ge(sup_rounded, n - 1)
                    if t < 4:
                        make_h(b + 1, bank_mix, 2 * t + 1)
                    else:
                        s2_rows(b + 1, 1 - u, 1)
                if live(b, t, -3):
                    if k == 0:
                        wait(pe, r2_done, b * T - T + 8)
                    accumulate((t - 1) % 2, k, 1)

            steps(pe, step)


def kernel(x, adj, L0_gnn_W, L0_gnn_a, L0_gnn_beta, L1_gnn_weight, L1_gnn_bias):
    import numpy as np
    import concourse.bacc as bacc
    from concourse.bass_utils import run_bass_kernel_spmd

    x = np.asarray(x)
    adj = np.asarray(adj)
    pairs = B * PAIRS
    arrays = {
        "x_d": x.reshape(pairs, 2, P, D).transpose(0, 2, 1, 3),
        "xT_d": x.reshape(pairs, 2 * P, C, P).transpose(0, 3, 2, 1),
        "adj_d": adj.reshape(T, P, N),
        "adjT_d": adj.T.reshape(T, P, N),
        "W0_d": np.asarray(L0_gnn_W).reshape(C, P, D).transpose(1, 0, 2),
        "a_d": np.asarray(L0_gnn_a).reshape(1, 2 * D),
        "beta_d": np.asarray(L0_gnn_beta).reshape(1, 1),
        "W1_d": np.asarray(L1_gnn_weight).reshape(C, P, D).transpose(1, 0, 2),
        "bias_d": np.asarray(L1_gnn_bias).reshape(1, D),
    }
    arrays = {name: np.ascontiguousarray(v) for name, v in arrays.items()}
    nc = bacc.Bacc("TRN2", target_bir_lowering=False, num_devices=1)
    args = [nc.dram_tensor(name, v.shape, mybir.dt.from_np(v.dtype), kind="ExternalInput").ap()
            for name, v in arrays.items()]
    out = nc.dram_tensor("out_d", (pairs, P, 2, D), F32, kind="ExternalOutput").ap()
    build(nc, *args, out)
    result = run_bass_kernel_spmd(nc, [arrays], core_ids=[0]).results[0]["out_d"]
    return np.ascontiguousarray(result.transpose(0, 2, 1, 3)).reshape(B, N, D)
```

```python
from contextlib import ExitStack

import concourse.bass as bass
import concourse.mybir as mybir

F32 = mybir.dt.float32
F32R = mybir.dt.float32r
ALU = mybir.AluOpType
ACT = mybir.ActivationFunctionType
AXX = mybir.AxisListType.X

P = 128
B, N, D = 8, 1024, 256
T = N // P
C = D // P
NT = B * T
HC = D + 2
PAIRS = T // 2
HALF = T // 2 * P
SLOPE = 0.2
EPS = 1e-5
TINY = 1.2e-38
ZR = 2
SR = 2
XS = 2 * T


def build(nc, x, xT, adj, adjT, W0, a, beta, W1, bias, out):
    with ExitStack() as ctx:
        def sb(name, shape, dt=F32):
            return ctx.enter_context(nc.sbuf_tensor(name, shape, dt))

        def pb(name):
            return ctx.enter_context(nc.psum_tensor(name, [P, 512], F32))

        def sem(name):
            return ctx.enter_context(nc.semaphore(name))

        def rings(columns):
            return [columns[:, i, :] for i in range(columns.shape[1])]

        adj_sb = sb("adj_sb", [P, T, N])
        adjT_hi = sb("adjT_hi", [P, T, N], F32R)
        adjT_lo = sb("adjT_lo", [P, T, N], F32R)
        w0_hi = sb("w0_hi", [P, C, HC], F32R)
        w0_lo = sb("w0_lo", [P, C, HC], F32R)
        w1_hi = sb("w1_hi", [P, C, D], F32R)
        w1_lo = sb("w1_lo", [P, C, D], F32R)
        ident = sb("ident", [P, P])
        beta_ident = sb("beta_ident", [P, P])
        bias_bc = sb("bias_bc", [P, D])
        beta_bc = sb("beta_bc", [P, 1])
        deg = sb("deg", [P, T])
        deg_pos = sb("deg_pos", [P, T])
        dis = sb("dis", [P, T])
        small = sb("small", [P, T // 2 + 6])
        neg_half, neg_one, eps, ones = (small[:, 0:T // 2], small[:, T // 2:T // 2 + 2],
                                        small[:, T // 2 + 2:T // 2 + 4], small[:, T // 2 + 4:T // 2 + 5])
        rest_max = small[0:1, T // 2 + 5:T // 2 + 6]
        rest_sum = sb("rest_sum", [P, T])
        rest_any = sb("rest_any", [P, T])
        need_rest = sb("need_rest", [1, 1], mybir.dt.int32)
        xT_sb = sb("xT_sb", [P, 2, C, 2 * P])
        xs_hi = sb("xs_hi", [P, C, 2 * P], F32R)
        xs_lo = sb("xs_lo", [P, C, 2 * P], F32R)
        h_hi = sb("h_hi", [P, 2, T, D], F32R)
        h_lo = sb("h_lo", [P, 2, T, D], F32R)
        s12 = sb("s12", [P, 2, T, 2])
        s2b = sb("s2b", [P, N])
        score = sb("score", [P, ZR, N])
        prob = sb("prob", [P, N])
        pt_hi = sb("pt_hi", [P, T, P], F32R)
        pt_lo = sb("pt_lo", [P, T, P], F32R)
        elu = sb("elu", [P, D])
        (neg_inv, row_max, neg_max, row_sum, inv_sum, var_eps, rstd, mean_rstd, shift) = rings(
            sb("per_row", [P, 9, SR]))
        o_var_eps, o_rstd, o_mean_rstd, o_shift = rings(sb("o_per_row", [P, 4, 4]))
        stats = sb("stats", [P, SR, 6])
        mv = sb("mv", [P, SR, 2])
        x1 = sb("x1", [P, XS, D])
        x1s_hi = sb("x1s_hi", [P, 2, D], F32R)
        x1s_lo = sb("x1s_lo", [P, 2, D], F32R)
        gt_hi = sb("gt_hi", [P, 2, C, HALF], F32R)
        gt_lo = sb("gt_lo", [P, 2, C, HALF], F32R)
        o_stats = sb("o_stats", [P, 2, 6])
        o_mv = sb("o_mv", [P, 2, 2])
        v12 = sb("v12", [P, C, 2])
        w0_raw = s2b[:, 0:C * D].rearrange("p (c d) -> p c d", c=C)
        a_bc = s2b[:, C * D:C * D + 2 * D]
        w1_raw = score[:, 1, 0:C * D].rearrange("p (c d) -> p c d", c=C)
        products = prob[:, :].rearrange("p (v d) -> p v d", v=2 * C)
        adjT_raw = [x1[:, T + 4 * k:T + 4 * k + 4, :].rearrange("p s d -> p (s d)") for k in range(2)]

        bank_pt = [pb("bank_pt0"), pb("bank_pt1")]
        bank_att = pb("bank_att")
        bank_mix = pb("bank_mix")
        bank_acc = [pb(f"bank_acc{i}") for i in range(4)]

        bank_h0 = bank_acc + bank_pt + [bank_att, bank_mix]

        x_in = [sem(f"x_in{s}") for s in range(XS // 2)]
        out_done = [sem(f"out_done{s}") for s in range(XS // 2)]
        xT_in = [sem(f"xT_in{q}") for q in range(2)]
        adj_in = [sem(f"adj_in{t}") for t in range(T)]
        adjT_in = [sem(f"adjT_in{k}") for k in range(2)]
        w0_in, w1_in, bias_in, beta_in, a_in = (
            sem("w0_in"), sem("w1_in"), sem("bias_in"), sem("beta_in"), sem("a_in"))
        const_done = sem("const_done")
        v_done, w0_rounded, w1_rounded, w_split = sem("v_done"), sem("w0_rounded"), sem("w1_rounded"), sem("w_split")
        beta_done = sem("beta_done")
        adjT_rounded, adjT_split, adjT_checked = sem("adjT_rounded"), sem("adjT_split"), sem("adjT_checked")
        rest_any_done, rest_count_done, rest_max_done, need_rest_ready = (
            sem("rest_any_done"), sem("rest_count_done"), sem("rest_max_done"), sem("need_rest_ready"))
        deg_done, deg_clamped, deg_rooted, dis_ready = (
            sem("deg_done"), sem("deg_clamped"), sem("deg_rooted"), sem("dis_ready"))
        x_rounded, x_split, x_first_split = sem("x_rounded"), sem("x_split"), sem("x_first_split")
        h_done, h_rounded, h_split = sem("h_done"), sem("h_rounded"), sem("h_split")
        s_ready, s2row_done, s2b_ready = sem("s_ready"), sem("s2row_done"), sem("s2b_ready")
        z_ready, leaky_done, max_done, negmax_done = (
            sem("z_ready"), sem("leaky_done"), sem("max_done"), sem("negmax_done"))
        exp_done, inv_done, prob_ready = sem("exp_done"), sem("inv_done"), sem("prob_ready")
        pt_done, pt_rounded, pt_split = sem("pt_done"), sem("pt_rounded"), sem("pt_split")
        att_done, eu_done, em_done, elu_done = sem("att_done"), sem("eu_done"), sem("em_done"), sem("elu_done")
        r_done, stats_done, mv_done, ve_done = sem("r_done"), sem("stats_done"), sem("mv_done"), sem("ve_done")
        rstd_done, x1_ready, x1b_done = sem("rstd_done"), sem("x1_ready"), sem("x1b_done")
        mean_rstd_done, shift_done = sem("mean_rstd_done"), sem("shift_done")
        omean_rstd_done, oshift_done = sem("omean_rstd_done"), sem("oshift_done")
        last_result_ready = sem("last_result_ready")
        x1s_done = sem("x1s_done")
        x1s_rounded, x1s_split, x1s_used = sem("x1s_rounded"), sem("x1s_split"), sem("x1s_used")
        gt_rounded, gt_split, product_done = sem("gt_rounded"), sem("gt_split"), sem("product_done")
        acc_done, r2_done, ostats_done, omv_done, ove_done, orstd_done, result_ready = (
            sem("acc_done"), sem("r2_done"), sem("ostats_done"), sem("omv_done"), sem("ove_done"),
            sem("orstd_done"), sem("result_ready"))

        def wait(eng, signal, count):
            if not isinstance(count, int) or count > 0:
                eng.wait_ge(signal, count)

        def live(b, t, shift=0):
            return not isinstance(b, int) or 0 <= T * b + t + shift < NT

        def batch_live(b):
            return not isinstance(b, int) or 0 <= b < B

        def steps(eng, step):
            for g in range(-T // 2, T):
                step(g // T, g // T // 2, g // T % 2, g % T)
            with eng.Fori(0, (B - 2) // 2) as i:
                for b, half, u in ((i * 2 + 1, i, 1), (i * 2 + 2, i + 1, 0)):
                    for t in range(T):
                        step(b, half, u, t)
            for b in (B - 1, B):
                for t in range(T):
                    step(b, b // 2, b % 2, t)

        def x0_part(buffer, q):
            return buffer[:, q // 2, :, q % 2 * 2 * P:(q % 2 + 1) * 2 * P]

        def deg_group(b, t):
            return {-1: 0, 3: 1}.get(T * b + t) if isinstance(b, int) else None

        def slot(u, t, shift=0):
            return (T * u + t + shift) % XS

        def out_bank(b, q):
            return [bank_mix, bank_att, *bank_pt][q if isinstance(b, int) and b == B else 0]

        def last_pair(b, q):
            return isinstance(b, int) and b * PAIRS + q == B * PAIRS - 1

        def adjT_step(b, t):
            k = T * b + t + 3 if isinstance(b, int) else -1
            return k if 0 <= k < T else None

        def deg_steps(b, t):
            m = T * b + t + T // 2 if isinstance(b, int) else T
            return (m,) if m < T else ()

        block = ctx.enter_context(nc.Block())

        @block.sync
        def _(sp):
            def load_xT(b, q):
                m = b * PAIRS + q
                if isinstance(b, int) and b == 0:
                    wait(sp, x_split, m - 1)
                else:
                    sp.wait_ge(h_done, 2 * (m - 1))
                sp.dma_start(xT_sb[:, q % 2, :, :], xT[m]).then_inc(xT_in[q % 2], 16)

            def load_x(b, u, q):
                s = slot(u, 2 * q)
                sp.dma_start(x1[:, s:s + 2, :], x[b * PAIRS + q]).then_inc(x_in[s // 2], 16)

            def load_adj(t):
                sp.dma_start(adj_sb[:, t, :], adj[t]).then_inc(adj_in[t], 16)

            def load_adjT(k):
                sp.dma_start(adjT_raw[k % 2], adjT[k]).then_inc(adjT_in[k % 2], 16)

            def round_(b, half_before, u):
                for c, q in ((b + 1, 2), (b + 1, 3), (b + 2, 0), (b + 2, 1)):
                    if batch_live(c):
                        load_xT(c, q)
                for q in range(PAIRS):
                    s = slot(1 - u, 2 * q)
                    if batch_live(b - 1):
                        sp.wait_ge(result_ready, (b - 1) * PAIRS + q + 3)
                        if last_pair(b - 1, q):
                            sp.wait_ge(last_result_ready, 1)
                        sp.dma_start(out[(b - 1) * PAIRS + q], x1[:, s:s + 2, :]).then_inc(out_done[s // 2], 16)
                for q in range(PAIRS):
                    s = slot(1 - u, 2 * q)
                    if batch_live(b - 1) and batch_live(b + 1):
                        sp.wait_ge(out_done[s // 2], (half_before + 1) * 16)
                        load_x(b + 1, 1 - u, q)

            load_xT(0, 0)
            sp.dma_start(w0_raw, W0).then_inc(w0_in, 16)
            sp.dma_start(a_bc, a.to_broadcast([P, 2 * D])).then_inc(a_in, 16)
            load_xT(0, 1)
            sp.dma_start(beta_bc[:, :], beta.to_broadcast([P, 1])).then_inc(beta_in, 16)
            sp.dma_start(w1_raw, W1).then_inc(w1_in, 16)
            sp.dma_start(bias_bc[:, :], bias.to_broadcast([P, D])).then_inc(bias_in, 16)
            load_adj(0)
            load_xT(0, 2)
            load_xT(0, 3)
            for t in range(1, T // 2):
                load_adj(t)
            load_adjT(0)
            load_adj(4)
            load_adjT(1)
            load_adj(5)
            load_x(0, 0, 0)
            load_xT(1, 0)
            load_xT(1, 1)
            load_adj(6)
            load_x(0, 0, 1)
            load_adj(7)
            load_x(0, 0, 2)
            load_x(0, 0, 3)
            for k in range(2, T):
                sp.wait_ge(adjT_checked, k - 1)
                load_adjT(k)
                if k in (2, 3):
                    load_xT(1, k)
            load_xT(2, 0)
            load_xT(2, 1)
            sp.wait_ge(adjT_checked, T)
            for q in range(PAIRS):
                load_x(1, 1, q)
            with sp.Fori(0, (B - 4) // 2) as i:
                round_(i * 2 + 1, i, 1)
                round_(i * 2 + 2, i, 0)
            for b in range(B - 3, B + 1):
                round_(b, (b - 1) // 2, b % 2)
            for s in range(XS // 2):
                sp.wait_ge(out_done[s], 16 * (B // 2))

        @block.gpsimd
        def _(pool):
            pool.memset(neg_half[:, :], -0.5).then_inc(omean_rstd_done, 1)
            pool.memset(neg_one[:, :], -1.0).then_inc(result_ready, 2)
            pool.memset(ones[:, :], 1.0)
            pool.memset(eps[:, :], EPS)
            pool.memset(ident[:, :], 0.0).then_inc(const_done, 1)
            pool.wait_ge(const_done, 1)
            pool.affine_select(out=ident[:, :], in_=ident[:, :], compare_op=ALU.not_equal, fill=1.0, base=0,
                               pattern=[[-1, P]], channel_multiplier=1).then_inc(const_done, 1)
            pool.wait_ge(const_done, 2)

            def rest_of_x(b, q):
                cols = slice(P if q == 0 else 0, 2 * P)
                pool.wait_ge(x_rounded, b * PAIRS + q + 1)
                pool.tensor_tensor(xs_lo[:, :, cols], xT_sb[:, q % 2, :, cols], xs_hi[:, :, cols].bitcast(F32),
                                   ALU.subtract).then_inc(x_split, 1)

            def step(b, half, u, t):
                n = b * T + t
                if batch_live(b + 1) and t == 0:
                    rest_of_x(b + 1, 0)
                if live(b, t, -2):
                    k, s = (t - 2) % T, slot(u, t, -2)
                    wait(pool, x1s_used, n - 3)
                    if isinstance(b, int) and n in (2, 6):
                        pool.wait_ge(dis_ready, n // 4 + 1)
                    pool.wait_ge(x1_ready, n - 1)
                    if live(b, t, -1):
                        pool.wait_ge(r_done, n)
                    pool.tensor_tensor(elu[:, :], x1[:, s, :], dis[:, k:k + 1].to_broadcast([P, D]),
                                       ALU.mult).then_inc(x1s_done, 1)
                    pool.wait_ge(x1s_rounded, n - 1)
                    pool.wait_ge(x1s_done, n - 1)
                    pool.tensor_tensor(x1s_lo[:, t % 2, :], elu[:, :], x1s_hi[:, t % 2, :].bitcast(F32),
                                       ALU.subtract).then_inc(x1s_split, 1)
                if live(b, t, -1):
                    k = (t - 1) % SR
                    one = slice(k, k + 1)
                    pool.wait_ge(mv_done, n)
                    pool.tensor_tensor(var_eps[:, one], mv[:, k, 1:2], eps[:, 0:1], ALU.add).then_inc(ve_done, 1)
                    pool.wait_ge(ve_done, n)
                    pool.tensor_tensor(rstd[:, one], var_eps[:, one], neg_half[:, 0:1], ALU.pow).then_inc(rstd_done, 1)
                    pool.wait_ge(rstd_done, n)
                    pool.tensor_tensor(mean_rstd[:, one], mv[:, k, 0:1], rstd[:, one],
                                       ALU.mult).then_inc(mean_rstd_done, 1)
                    pool.wait_ge(mean_rstd_done, n)
                    pool.tensor_tensor(shift[:, one], mean_rstd[:, one], neg_one[:, 0:1],
                                       ALU.mult).then_inc(shift_done, 1)
                if batch_live(b + 1) and t < 3:
                    rest_of_x(b + 1, t + 1)
                if batch_live(b - 1) and t >= 4:
                    m = (b - 1) * PAIRS + t - 3
                    two = slice(t % 2 * 2, t % 2 * 2 + 2)
                    pool.wait_ge(result_ready, m)
                    pool.wait_ge(omv_done, 2 * m)
                    pool.tensor_tensor(o_var_eps[:, two], o_mv[:, :, 1], eps[:, :], ALU.add).then_inc(ove_done, 1)
                    pool.wait_ge(ove_done, m)
                    pool.tensor_tensor(o_rstd[:, two], o_var_eps[:, two], neg_half[:, 0:2],
                                       ALU.pow).then_inc(orstd_done, 1)
                    pool.wait_ge(orstd_done, m)
                    pool.tensor_tensor(o_mean_rstd[:, two], o_mv[:, :, 0], o_rstd[:, two],
                                       ALU.mult).then_inc(omean_rstd_done, 1)
                    pool.wait_ge(omean_rstd_done, m + 1)
                    pool.tensor_tensor(o_shift[:, two], o_mean_rstd[:, two], neg_one[:, :],
                                       ALU.mult).then_inc(oshift_done, 1)
                if live(b, t, 2):
                    k = (t + 2) % SR
                    pool.wait_ge(max_done, n + 3)
                    pool.tensor_tensor(neg_max[:, k:k + 1], row_max[:, k:k + 1], neg_one[:, 0:1],
                                       ALU.mult).then_inc(negmax_done, 1)
                if live(b, t):
                    s = slot(u, t)
                    pool.wait_ge(x_in[s // 2], (half + 1) * 16)
                    pool.wait_ge(elu_done, n + 1)
                    pool.tensor_tensor(x1[:, s, :], x1[:, s, :], elu[:, :], ALU.subtract).then_inc(r_done, 1)
                if live(b, t, -2):
                    s = slot(u, t, -2)
                    if isinstance(b, int) and n == 2:
                        pool.wait_ge(bias_in, 16)
                    pool.wait_ge(x1s_split, n - 1)
                    pool.tensor_tensor(x1[:, s, :], x1[:, s, :], bias_bc[:, :], ALU.add).then_inc(x1b_done, 1)
                k = adjT_step(b, t - 1)
                if k is not None:
                    pool.wait_ge(adjT_rounded, k + 1)
                    pool.tensor_tensor(adjT_lo[:, k, :], adjT_raw[k % 2], adjT_hi[:, k, :].bitcast(F32),
                                       ALU.subtract).then_inc(adjT_split, 1)
                i = deg_group(b, t)
                if i is not None:
                    cols = slice(4 * i, 4 * i + 4)
                    pool.wait_ge(deg_clamped, i + 1)
                    pool.tensor_tensor(dis[:, cols], deg[:, cols], neg_half[:, :], ALU.pow).then_inc(deg_rooted, 1)

            steps(pool, step)

        @block.scalar
        def _(act):
            act.wait_ge(w0_in, 16)
            nc.scalar.activation(w0_hi[:, :, 0:D], w0_raw, ACT.Copy).then_inc(w0_rounded, 1)
            act.wait_ge(v_done, 1)
            nc.scalar.activation(w0_hi[:, :, D:HC], v12[:, :, :], ACT.Copy).then_inc(w0_rounded, 1)

            def round_h(b, par, m, bank):
                act.wait_ge(h_done, b * T + m + 1)
                nc.scalar.activation(h_hi[:, par, m, :], bank[:, 0:D], ACT.Copy).then_inc(h_rounded, 1)

            def normalize_out(b, u, q):
                act.wait_ge(oshift_done, b * PAIRS + q + 1)
                for i in range(1 if last_pair(b, q) else 2):
                    s = slot(u, 2 * q + i)
                    last = nc.scalar.activation(x1[:, s, :], x1[:, s, :], ACT.Identity,
                                                scale=o_rstd[:, q % 2 * 2 + i:q % 2 * 2 + i + 1],
                                                bias=o_shift[:, q % 2 * 2 + i:q % 2 * 2 + i + 1])
                last.then_inc(result_ready, 1)

            def round_gt(b, i):
                if i == 0:
                    act.wait_ge(acc_done, b + 1)
                else:
                    act.wait_ge(x1s_used, b * T + T)
                for c in range(C):
                    nc.scalar.activation(gt_hi[:, i, c, :], bank_acc[2 * i + c][:, :], ACT.Copy).then_inc(gt_rounded, 1)

            def copy_s2(b, i):
                if i == 0:
                    wait(act, z_ready, b * T)
                act.wait_ge(s2row_done, b * 2 + i + 1)
                nc.scalar.activation(s2b[:, i * HALF:(i + 1) * HALF], bank_mix[:, :], ACT.Copy).then_inc(s2b_ready, 1)

            for m in range(T):
                round_h(0, 0, m, bank_h0[m])
            act.wait_ge(w1_in, 16)
            nc.scalar.activation(w1_hi[:, :, :], w1_raw, ACT.Copy).then_inc(w1_rounded, 1)

            def step(b, half, u, t):
                n = b * T + t
                if live(b, t, -2):
                    k, s = (t - 2) % T, slot(u, t, -2)
                    if isinstance(b, int) and n in (2, 6):
                        act.wait_ge(dis_ready, n // 4 + 1)
                    wait(act, x1s_used, n - 3)
                    act.wait_ge(x1_ready, n - 1)
                    nc.scalar.activation(x1s_hi[:, t % 2, :], x1[:, s, :], ACT.Copy,
                                         scale=dis[:, k:k + 1]).then_inc(x1s_rounded, 1)
                if live(b, t, 1):
                    k = (t + 1) % SR
                    wait(act, pt_done, n * 2 + 2)
                    act.wait_ge(negmax_done, n + 2)
                    nc.scalar.activation(prob[:, :], score[:, k % ZR, :], ACT.Exp,
                                         bias=neg_max[:, k:k + 1],
                                         accum_out=row_sum[:, k:k + 1]).then_inc(exp_done, 1)
                k = adjT_step(b, t - 2)
                if k is not None:
                    act.wait_ge(adjT_split, k + 1)
                    nc.scalar.activation(adjT_raw[k % 2], adjT_lo[:, k, :].bitcast(F32), ACT.Abs,
                                         accum_out=rest_sum[:, k:k + 1]).then_inc(adjT_checked, 1)
                if batch_live(b + 1) and t < 4:
                    for j in range(2):
                        round_h(b + 1, 1 - u, 2 * t + j, bank_pt[j])
                if batch_live(b - 1) and t == 2:
                    round_gt(b - 1, 0)
                if batch_live(b + 1) and t == 5:
                    copy_s2(b + 1, 0)
                if live(b, t):
                    act.wait_ge(att_done, n + 1)
                    wait(act, r_done, n)
                    if live(b, t, -2):
                        act.wait_ge(x1s_split, n - 1)
                    nc.scalar.activation(elu[:, :], bank_att[:, 0:D], ACT.Exp,
                                         scale=inv_sum[:, t % SR:t % SR + 1]).then_inc(eu_done, 1)
                    act.wait_ge(eu_done, n + 1)
                    nc.scalar.activation(elu[:, :], elu[:, :], ACT.Relu, scale=-1.0,
                                         bias=ones[:, :]).then_inc(em_done, 1)
                if batch_live(b + 1) and t == 5:
                    copy_s2(b + 1, 1)
                if live(b, t, 1):
                    for i in range(2):
                        act.wait_ge(pt_done, n * 2 + 3 + i)
                        nc.scalar.activation(pt_hi[:, 4 * i:4 * i + 4, :], bank_pt[i][:, :].rearrange(
                            "p (k q) -> p k q", k=4), ACT.Copy).then_inc(pt_rounded, 1)
                if live(b, t, -1):
                    k, s = (t - 1) % SR, slot(u, t, -1)
                    act.wait_ge(shift_done, n)
                    nc.scalar.activation(x1[:, s, :], x1[:, s, :], ACT.Identity, scale=rstd[:, k:k + 1],
                                         bias=shift[:, k:k + 1]).then_inc(x1_ready, 1)
                if live(b, t, 3):
                    tz = (t + 3) % T
                    par = u if t + 3 < T else 1 - u
                    if tz == 0:
                        act.wait_ge(s2b_ready, b * 2 + 4)
                    if isinstance(b, int) and n == -2:
                        act.wait_ge(w_split, 3)
                    wait(act, exp_done, n + 2)
                    nc.scalar.activation(score[:, (t + 3) % ZR, :], s2b[:, :], ACT.Identity,
                                         bias=s12[:, par, tz, 0:1]).then_inc(z_ready, 1)
                if batch_live(b - 1) and t >= 4:
                    normalize_out(b - 1, 1 - u, t - 4)
                if batch_live(b - 1) and t == 2:
                    round_gt(b - 1, 1)

            steps(act, step)

        @block.vector
        def _(dve):
            dve.memset(row_max[:, :], 0.0)

            def split_x(b, q):
                m = b * PAIRS + q
                dve.wait_ge(xT_in[q % 2], (b * 2 + q // 2 + 1) * 16)
                if isinstance(b, int) and b == 0:
                    dve.tensor_copy(x0_part(gt_hi, q), xT_sb[:, q % 2, :, :]).then_inc(x_rounded, 1)
                    dve.wait_ge(x_rounded, m + 1)
                    dve.tensor_tensor(x0_part(gt_lo, q), xT_sb[:, q % 2, :, :],
                                      x0_part(gt_hi, q).bitcast(F32), ALU.subtract).then_inc(x_split, 1)
                else:
                    dve.wait_ge(h_done, 2 * m)
                    dve.tensor_copy(xs_hi[:, :, :], xT_sb[:, q % 2, :, :]).then_inc(x_rounded, 1)
                    if q == 0:
                        dve.wait_ge(x_rounded, m + 1)
                        dve.tensor_tensor(xs_lo[:, :, 0:P], xT_sb[:, 0, :, 0:P], xs_hi[:, :, 0:P].bitcast(F32),
                                          ALU.subtract).then_inc(x_first_split, 1)

            split_x(0, 0)
            dve.wait_ge(w0_in, 16)
            dve.wait_ge(a_in, 16)
            for c in range(C):
                for j in range(2):
                    last = dve.tensor_tensor_reduce(out=products[:, 2 * c + j, :], in0=w0_raw[:, c, :],
                                                    in1=a_bc[:, j * D:(j + 1) * D], scale=1.0, scalar=0.0, op0=ALU.mult, op1=ALU.add,
                                                    accum_out=v12[:, c, j:j + 1])
            last.then_inc(v_done, 1)
            dve.wait_ge(w0_rounded, 1)
            dve.tensor_tensor(w0_lo[:, :, 0:D], w0_raw, w0_hi[:, :, 0:D].bitcast(F32), ALU.subtract).then_inc(w_split, 1)
            dve.wait_ge(w0_rounded, 2)
            dve.tensor_tensor(w0_lo[:, :, D:HC], v12[:, :, :], w0_hi[:, :, D:HC].bitcast(F32),
                              ALU.subtract).then_inc(w_split, 1)

            def rest_of_h(b, par, m, bank):
                dve.wait_ge(h_rounded, b * T + m + 1)
                dve.tensor_copy(s12[:, par, m, :], bank[:, D:HC]).then_inc(s_ready, 1)
                dve.tensor_tensor(h_lo[:, par, m, :], bank[:, 0:D], h_hi[:, par, m, :].bitcast(F32),
                                  ALU.subtract).then_inc(h_split, 1)

            def rest_of_gt(b, i):
                for c in range(C):
                    dve.wait_ge(gt_rounded, b * 4 + 2 * i + c + 1)
                    dve.tensor_tensor(gt_lo[:, i, c, :], bank_acc[2 * i + c][:, :], gt_hi[:, i, c, :].bitcast(F32),
                                      ALU.subtract).then_inc(gt_split, 1)

            def residual(b, u, q, bank):
                if q == 0:
                    dve.wait_ge(x1b_done, b * T + T)
                dve.wait_ge(product_done, b * PAIRS + q + 1)
                for j in range(2):
                    m = 2 * q + j
                    s = slot(u, m)
                    dve.scalar_tensor_tensor(out=x1[:, s, :], in0=bank[:, j * D:(j + 1) * D],
                                             scalar=dis[:, m:m + 1], in1=x1[:, s, :], op0=ALU.mult,
                                             op1=ALU.add).then_inc(r2_done, 1)

            def scale_prob(b, t):
                n = b * T + t
                k, m = (t + 1) % SR, (t + 1) % T
                dve.wait_ge(exp_done, n + 2)
                dve.reciprocal(inv_sum[:, k:k + 1], row_sum[:, k:k + 1]).then_inc(inv_done, 1)
                if isinstance(b, int) and n == -1:
                    dve.wait_ge(beta_done, 1)
                dve.scalar_tensor_tensor(out=prob[:, m * P:(m + 1) * P], in0=beta_ident[:, :],
                                         scalar=row_sum[:, k:k + 1], in1=prob[:, m * P:(m + 1) * P],
                                         op0=ALU.mult, op1=ALU.add).then_inc(prob_ready, 1)

            def leaky_of(b, t):
                n = b * T + t
                k = (t + 2) % ZR
                dve.wait_ge(z_ready, n + 3)
                dve.scalar_tensor_tensor(out=score[:, k, :], in0=score[:, k, :], scalar=SLOPE,
                                         in1=score[:, k, :], op0=ALU.mult, op1=ALU.max).then_inc(leaky_done, 1)

            def elu_of(b, t):
                n = b * T + t
                e = elu[:, :]
                dve.wait_ge(em_done, n + 1)
                dve.scalar_tensor_tensor(out=e, in0=bank_att[:, 0:D], scalar=neg_inv[:, t % SR:t % SR + 1],
                                         in1=e, op0=ALU.mult, op1=ALU.min).then_inc(elu_done, 1)

            def step(b, half, u, t):
                n = b * T + t
                out_pair = batch_live(b - 1) and t >= 4
                if batch_live(b + 1) and t == 0:
                    split_x(b + 1, 0)
                if out_pair:
                    q = t - 4
                    residual(b - 1, 1 - u, q, out_bank(b, q))
                    if live(b, t, -1):
                        dve.wait_ge(stats_done, n)
                    for i in range(2):
                        s = slot(1 - u, 2 * q + i)
                        dve.wait_ge(r2_done, b * T - T + 2 * q + i + 1)
                        dve.bn_stats(o_stats[:, i, :], x1[:, s, :]).then_inc(ostats_done, 1)
                if live(b, t, -1) and t >= 4:
                    if not out_pair:
                        dve.wait_ge(stats_done, n)
                    dve.bn_aggr(mv[:, (t - 1) % SR, :], stats[:, (t - 1) % SR, :]).then_inc(mv_done, 1)
                if out_pair:
                    dve.wait_ge(omean_rstd_done, b * PAIRS - PAIRS + q + 1)
                    dve.wait_ge(ostats_done, b * T - T + 2 * q + 2)
                if live(b, t, 1) and t >= 4:
                    scale_prob(b, t)
                if batch_live(b - 1) and t == 3:
                    rest_of_gt(b - 1, 1)
                if live(b, t, -1) and t < 4:
                    dve.wait_ge(stats_done, n)
                if live(b, t, 2):
                    leaky_of(b, t)
                if out_pair:
                    for i in range(2):
                        dve.bn_aggr(o_mv[:, i, :], o_stats[:, i, :]).then_inc(omv_done, 1)
                if live(b, t, -1) and t < 4:
                    dve.bn_aggr(mv[:, (t - 1) % SR, :], stats[:, (t - 1) % SR, :]).then_inc(mv_done, 1)
                if live(b, t, 1) and t < 4:
                    scale_prob(b, t)
                if batch_live(b + 1) and t < 4:
                    for j in range(2):
                        rest_of_h(b + 1, 1 - u, 2 * t + j, bank_pt[j])
                    if t < 3:
                        split_x(b + 1, t + 1)
                if live(b, t, 1):
                    k = (t + 1) % SR
                    if live(b, t, 2):
                        dve.wait_ge(leaky_done, n + 3)
                    dve.wait_ge(inv_done, n + 2)
                    dve.tensor_scalar(neg_inv[:, k:k + 1], inv_sum[:, k:k + 1], -1.0, None, ALU.mult)
                if isinstance(b, int) and n == T - 2:
                    dve.wait_ge(adjT_checked, T)
                    dve.tensor_scalar(rest_any[:, :], rest_sum[:, :], 0.0, None,
                                      ALU.not_equal).then_inc(rest_any_done, 1)
                if live(b, t) and t >= 6:
                    elu_of(b, t)
                if live(b, t, 2):
                    k = (t + 2) % SR
                    m = (t + 2) % T
                    if isinstance(b, int) and n + 2 < T:
                        dve.wait_ge(adj_in[m], 16)
                    if not live(b, t, 1):
                        dve.wait_ge(leaky_done, n + 3)
                    dve.tensor_tensor_reduce(out=score[:, k % ZR, :], in0=score[:, k % ZR, :], in1=adj_sb[:, m, :],
                                             scale=1.0, scalar=-3.4e38, op0=ALU.mult, op1=ALU.max,
                                             accum_out=row_max[:, k:k + 1]).then_inc(max_done, 1)
                if batch_live(b - 1) and t == 2:
                    rest_of_gt(b - 1, 0)
                if live(b, t) and t < 6:
                    elu_of(b, t)
                if live(b, t, 1):
                    for i in range(2):
                        dve.wait_ge(pt_rounded, n * 2 + 3 + i)
                        dve.tensor_tensor(pt_lo[:, 4 * i:4 * i + 4, :], bank_pt[i][:, :].rearrange(
                            "p (k q) -> p k q", k=4), pt_hi[:, 4 * i:4 * i + 4, :].bitcast(F32),
                            ALU.subtract).then_inc(pt_split, 1)
                if isinstance(b, int) and n == T - 2:
                    dve.wait_ge(rest_count_done, 1)
                    dve.reduce_max(rest_max[:, :], bank_mix[0:1, 0:T], AXX).then_inc(rest_max_done, 1)
                    dve.wait_ge(rest_max_done, 1)
                    dve.tensor_scalar(need_rest[:, :], rest_max[:, :], 0.0, None, ALU.is_gt).then_inc(need_rest_ready, 1)
                if live(b, t):
                    k = t % SR
                    dve.wait_ge(r_done, n + 1)
                    dve.bn_stats(stats[:, k, :], x1[:, slot(u, t), :]).then_inc(stats_done, 1)
                for m in deg_steps(b, t):
                    dve.wait_ge(adj_in[m], 16)
                    dve.reduce_sum(deg[:, m:m + 1], adj_sb[:, m, :], AXX).then_inc(deg_done, 1)
                i = deg_group(b, t)
                if i is not None:
                    cols = slice(4 * i, 4 * i + 4)
                    dve.wait_ge(deg_done, 4 * i + 4)
                    dve.tensor_scalar(deg_pos[:, cols], deg[:, cols], 0.0, None, ALU.is_gt)
                    dve.tensor_scalar(deg[:, cols], deg[:, cols], TINY, None, ALU.max).then_inc(deg_clamped, 1)
                i = deg_group(b, t - 1)
                if i is not None:
                    cols = slice(4 * i, 4 * i + 4)
                    dve.wait_ge(deg_rooted, i + 1)
                    dve.tensor_tensor(dis[:, cols], dis[:, cols], deg_pos[:, cols], ALU.mult).then_inc(dis_ready, 1)
                k = adjT_step(b, t)
                if k is not None:
                    dve.wait_ge(adjT_in[k % 2], 16 * (k // 2 + 1))
                    dve.tensor_copy(adjT_hi[:, k, :], adjT_raw[k % 2]).then_inc(adjT_rounded, 1)

            for q in range(PAIRS):
                if q:
                    split_x(0, q)
                if q > 1:
                    for m in (2 * q - 4, 2 * q - 3):
                        rest_of_h(0, 0, m, bank_h0[m])
            for m in range(T // 2, T):
                rest_of_h(0, 0, m, bank_h0[m])
            dve.wait_ge(w1_rounded, 1)
            dve.tensor_tensor(w1_lo[:, :, :], w1_raw, w1_hi[:, :, :].bitcast(F32), ALU.subtract).then_inc(w_split, 1)
            dve.wait_ge(const_done, 2)
            dve.wait_ge(beta_in, 16)
            dve.tensor_scalar(beta_ident[:, :], ident[:, :], beta_bc[:, :], None, ALU.mult).then_inc(beta_done, 1)
            steps(dve, step)
            dve.wait_ge(oshift_done, B * PAIRS)
            dve.tensor_scalar(x1[:, XS - 1, :], x1[:, XS - 1, :], o_rstd[:, 3:4], o_shift[:, 3:4], ALU.mult,
                              ALU.add).then_inc(last_result_ready, 1)

        @block.tensor
        def _(pe):
            def product(bank, lhs, rhs, pieces, first=True, last=True, skip=False):
                passes = [(l, r, p) for p in pieces for l, r in ((0, 0), (0, 1), (1, 0))]
                for j, (l, r, p) in enumerate(passes):
                    mm = pe.matmul(bank, lhs[l](p), rhs[r](p), start=first and j == 0,
                                   stop=last and j == len(passes) - 1, skip_group_check=skip)
                return mm

            def make_h(m, parts, bank):
                cols = slice(m % 2 * P, (m % 2 + 1) * P)
                product(bank[:, 0:HC], [lambda c, s=s: s[:, c, cols] for s in parts],
                        [lambda c, w=w: w[:, c, :] for w in (w0_hi, w0_lo)], range(C)).then_inc(h_done, 1)

            def s2_rows(b, par, i):
                if i == 0:
                    pe.wait_ge(s_ready, b * T + T)
                for j in range(4):
                    mm = pe.transpose(bank_mix[:, j * P:(j + 1) * P],
                                      s12[:, par, 4 * i + j, 1:2].to_broadcast([P, P]), ident[:, :])
                mm.then_inc(s2row_done, 1)

            def attend(u, i):
                return product(bank_att[:, 0:D], [lambda k, p=p: p[:, k, :] for p in (pt_hi, pt_lo)],
                               [lambda k, h=h: h[:, u, k, 0:D] for h in (h_hi, h_lo)],
                               range(4 * i, 4 * i + 4), first=i == 0, last=i == 1)

            def accumulate(l, r, k, par, i, first=False, last=False):
                for c in range(C):
                    mm = pe.matmul(bank_acc[2 * i + c][:, :], l[:, par, c * P:(c + 1) * P],
                                   r[:, k, i * HALF:(i + 1) * HALF], start=first and k == 0,
                                   stop=last and k == T - 1)
                return mm

            def times_w1(q, bank):
                for j in range(2):
                    cols = slice((q % 2 * 2 + j) * P, (q % 2 * 2 + j + 1) * P)
                    mm = product(bank[:, j * D:(j + 1) * D],
                                 [lambda c, g=g: g[:, q // 2, c, cols] for g in (gt_hi, gt_lo)],
                                 [lambda c, w=w: w[:, c, :] for w in (w1_hi, w1_lo)], range(C))
                mm.then_inc(product_done, 1)

            pe.wait_ge(w_split, 2)
            for q in range(PAIRS):
                pe.wait_ge(x_split, q + 1)
                for m in (2 * q, 2 * q + 1):
                    make_h(m, [x0_part(g, q) for g in (gt_hi, gt_lo)], bank_h0[m])
            pe.wait_ge(const_done, 2)
            need_rest_value = []

            def add_halves(b, n, halves):
                for k, par, i in halves:
                    if i == 0 and isinstance(b, int) and n - 2 < T:
                        pe.wait_ge(adjT_split, k + 1)
                    if k == 0:
                        wait(pe, gt_split, b * 4 - 2 + 2 * i)
                    if i == 0:
                        pe.wait_ge(x1s_split, n - 1)
                    accumulate(x1s_hi, adjT_hi, k, par, i, first=True)
                if isinstance(b, int) and b < 1:
                    for half in halves:
                        accumulate(x1s_hi, adjT_lo, *half)
                elif halves:
                    with pe.If(need_rest_value[0] != 0):
                        for half in halves:
                            accumulate(x1s_hi, adjT_lo, *half)
                for k, par, i in halves:
                    mm = accumulate(x1s_lo, adjT_hi, k, par, i, last=True)
                    if i == 1:
                        mm.then_inc(x1s_used, 1)
                    elif k == T - 1:
                        mm.then_inc(acc_done, 1)

            def step(b, half, u, t):
                n = b * T + t
                if live(b, t):
                    if t == 0:
                        pe.wait_ge(h_split, b * T + T)
                    wait(pe, elu_done, n)
                    pe.wait_ge(pt_split, n * 2 + 1)
                    attend(u, 0)
                if batch_live(b + 1) and t < 4:
                    if t == 0:
                        pe.wait_ge(x_first_split, b + 1)
                    else:
                        pe.wait_ge(x_split, b * PAIRS + PAIRS + t + 1)
                    make_h(2 * t, [xs_hi, xs_lo], bank_pt[0])
                    if t == 0:
                        pe.wait_ge(x_split, b * PAIRS + PAIRS + 1)
                    pe.wait_ge(pt_split, n * 2 + 2)
                    make_h(2 * t + 1, [xs_hi, xs_lo], bank_pt[1])
                if batch_live(b + 1) and t == 5:
                    if isinstance(b, int) and b < 0:
                        pe.wait_ge(h_split, T)
                    wait(pe, r2_done, b * T - T + 4)
                    s2_rows(b + 1, 1 - u, 0)
                if live(b, t):
                    pe.wait_ge(pt_split, n * 2 + 2)
                    attend(u, 1).then_inc(att_done, 1)
                if batch_live(b + 1) and t == 5:
                    pe.wait_ge(s2b_ready, b * 2 + 3)
                    s2_rows(b + 1, 1 - u, 1)
                if live(b, t, 1):
                    pe.wait_ge(prob_ready, n + 2)
                    for i in range(2):
                        if batch_live(b + 1) and t < 4:
                            pe.wait_ge(h_split, b * T + T + 2 * t + i + 1)
                        for j in range(4):
                            k = 4 * i + j
                            mm = pe.transpose(bank_pt[i][:, j * P:(j + 1) * P], prob[:, k * P:(k + 1) * P],
                                              ident[:, :])
                        mm.then_inc(pt_done, 1)
                if isinstance(b, int) and n == T - 2:
                    pe.wait_ge(rest_any_done, 1)
                    pe.wait_ge(s2b_ready, 4)
                    pe.matmul(bank_mix[0:1, 0:T], ones[:, :], rest_any[:, :], start=True,
                              stop=True).then_inc(rest_count_done, 1)
                last_tile = [((t - 3) % T, (t - 1) % 2, 1)] if live(b, t, -3) else []
                this_tile = [(((t - 2) % T), t % 2, 0)] if live(b, t, -2) else []
                for halves in (last_tile, this_tile) if t == 2 else (last_tile + this_tile,):
                    add_halves(b, n, halves)
                if batch_live(b - 1) and 3 <= t < 7:
                    q = t - 3
                    if isinstance(b, int) and b == B:
                        pe.wait_ge(elu_done, NT)
                    elif batch_live(b + 1) and t == 5:
                        pe.wait_ge(s2b_ready, b * 2 + 4)
                    elif t > 3:
                        pe.wait_ge(r2_done, b * T - T + 2 * q)
                    if q % 2 == 0:
                        pe.wait_ge(gt_split, b * 4 - 2 + q)
                    times_w1(q, out_bank(b, q))
                if isinstance(b, int) and n == T - 1:
                    pe.wait_ge(need_rest_ready, 1)
                    need_rest_value.append(pe.value_load(need_rest[0:1, 0:1], min_val=0, max_val=1))

            steps(pe, step)


def kernel(x, adj, L0_gnn_W, L0_gnn_a, L0_gnn_beta, L1_gnn_weight, L1_gnn_bias):
    import numpy as np
    import concourse.bacc as bacc
    from concourse.bass_utils import run_bass_kernel_spmd

    x = np.asarray(x)
    adj = np.asarray(adj)
    pairs = B * PAIRS
    arrays = {
        "x_d": x.reshape(pairs, 2, P, D).transpose(0, 2, 1, 3),
        "xT_d": x.reshape(pairs, 2 * P, C, P).transpose(0, 3, 2, 1),
        "adj_d": adj.reshape(T, P, N),
        "adjT_d": adj.T.reshape(T, P, N),
        "W0_d": np.asarray(L0_gnn_W).reshape(C, P, D).transpose(1, 0, 2),
        "a_d": np.asarray(L0_gnn_a).reshape(1, 2 * D),
        "beta_d": np.asarray(L0_gnn_beta).reshape(1, 1),
        "W1_d": np.asarray(L1_gnn_weight).reshape(C, P, D).transpose(1, 0, 2),
        "bias_d": np.asarray(L1_gnn_bias).reshape(1, D),
    }
    arrays = {name: np.ascontiguousarray(v) for name, v in arrays.items()}
    nc = bacc.Bacc("TRN2", target_bir_lowering=False, num_devices=1)
    args = [nc.dram_tensor(name, v.shape, mybir.dt.from_np(v.dtype), kind="ExternalInput").ap()
            for name, v in arrays.items()]
    out = nc.dram_tensor("out_d", (pairs, P, 2, D), F32, kind="ExternalOutput").ap()
    build(nc, *args, out)
    result = run_bass_kernel_spmd(nc, [arrays], core_ids=[0]).results[0]["out_d"]
    return np.ascontiguousarray(result.transpose(0, 2, 1, 3)).reshape(B, N, D)
```
